# Optimizing a Trainium2 kernel written in Bass

```python
import numpy as np
import jax
import jax.numpy as jnp

def _softmax(x, axis=-1):
    return jax.nn.softmax(x, axis=axis)

def _gelu(x):
    return jax.nn.gelu(x, approximate=True)

def _silu(x):
    return jax.nn.silu(x)

def _sigmoid(x):
    return jax.nn.sigmoid(x)

def _layernorm(x, axis=-1, eps=1e-05):
    m = jnp.mean(x, axis=axis, keepdims=True)
    v = jnp.var(x, axis=axis, keepdims=True)
    return (x - m) / jnp.sqrt(v + eps)

def _scatter_add(tgt, idx, src, axis=0):
    return tgt.at[idx].add(src)

def _segment_sum(src, seg, n):
    return jax.ops.segment_sum(src, seg, n)
kernel_name = 'mk_flamingo_gated_d2_seqx_r8_d9e3c0'

def setup_inputs(seed: int=0):
    np.random.seed(seed)
    _w = jnp.asarray

    def _rec_inputs():
        import jax
        import jax.numpy as jnp
        _rk = jax.random.key(seed)
        x = -0.0002928 + 1 * jax.random.normal(jax.random.fold_in(_rk, 1), (4, 256, 128), jnp.float32)
        _lenS = 256 - jax.random.randint(jax.random.fold_in(_rk, 7), (4,), 0, max(1, 256 // 4) + 1, jnp.int32)
        _lenS2 = 256 - jax.random.randint(jax.random.fold_in(_rk, 8), (4,), 0, max(1, 256 // 4) + 1, jnp.int32)
        _ctx_1024P = jax.random.normal(jax.random.fold_in(_rk, 11), (4, 16, 128), jnp.float32)
        _ctx_1024c = jax.random.dirichlet(jax.random.fold_in(_rk, 511), 0.3 * jnp.ones((16,), jnp.float32), (4, 256))
        _ctx_1024t = jnp.einsum('bsk,bkd->bsd', _ctx_1024c, _ctx_1024P)
        _ctx_1024t = _ctx_1024t * jax.lax.rsqrt(jnp.mean(jnp.square(_ctx_1024t)) + 1e-12) * 0.953939
        ctx_1024 = -1.39393e-06 + 0.999914 * (_ctx_1024t + 0.3 * jax.random.normal(jax.random.fold_in(_rk, 611), (4, 256, 128), jnp.float32))
        _g = jax.random.normal(jax.random.fold_in(_rk, 9001), (2, 2), jnp.float32)
        _g = jnp.sign(_g) * jnp.maximum(jnp.abs(_g), 1.0) + (_g == 0) * 1.0
        g_xattn = _g[0]
        g_ffn = _g[1]
        return (x, ctx_1024, g_xattn, g_ffn)
    x, ctx_1024, g_xattn, g_ffn = _rec_inputs()

    def _L0_xattn_setup():
        import jax, jax.numpy as jnp
        import numpy as np
        E_PHI = 128
        E_F = 128
        HID = 128
        N_HEADS = 16
        HEAD_DIM = HID // N_HEADS
        key = jax.random.key(seed)
        ks = jax.random.split(key, 9)
        B, S = (2, 256)
        s = 0.02
        return {'q': jax.random.normal(ks[0], (B, S, E_PHI), jnp.float32), 'k': jax.random.normal(ks[1], (B, S, E_PHI), jnp.float32), 'v': jax.random.normal(ks[2], (B, S, E_F), jnp.float32), 'W_q': jax.random.normal(ks[3], (E_PHI, HID), jnp.float32) * s, 'W_k': jax.random.normal(ks[4], (E_PHI, HID), jnp.float32) * s, 'W_v': jax.random.normal(ks[5], (E_F, HID), jnp.float32) * s, 'b_v': jax.random.normal(ks[6], (HID,), jnp.float32) * s, 'W_o': jax.random.normal(ks[7], (HID, E_F), jnp.float32) * s, 'b_o': jax.random.normal(ks[8], (E_F,), jnp.float32) * s}
    _L0_xattn_all = _L0_xattn_setup()
    _L0_xattn_in = {k: v for k, v in _L0_xattn_all.items() if k in ('W_q', 'W_k', 'W_v', 'b_v', 'W_o', 'b_o')}
    del _L0_xattn_all

    def _L0_ffn_setup():
        import jax, jax.numpy as jnp
        import numpy as np
        from jax import lax
        TOP_K = 1
        key = jax.random.key(seed)
        ks = jax.random.split(key, 9)
        B, N, C = (4, 256, 128)
        E, L, R = (6, 100, 16)
        return {'feats': jax.random.normal(ks[0], (B, N, C), jnp.float32), 'A': jax.random.normal(ks[1], (E, L, R), jnp.float32) * 0.05, 'B': jax.random.normal(ks[2], (E, R, C), jnp.float32) * 0.05, 'w_gate': jax.random.normal(ks[3], (C, E), jnp.float32) * 0.02, 'wt_w': jax.random.normal(ks[4], (C, C), jnp.float32) * (1.0 / np.sqrt(C)), 'wt_b': jax.random.normal(ks[5], (C,), jnp.float32) * 0.01, 'wd_w': jax.random.normal(ks[6], (C, C), jnp.float32) * (1.0 / np.sqrt(C)), 'wd_b': jax.random.normal(ks[7], (C,), jnp.float32) * 0.01, 'scale': jnp.full((1,), 0.001, jnp.float32)}
    _L0_ffn_all = _L0_ffn_setup()
    _L0_ffn_in = {k: v for k, v in _L0_ffn_all.items() if k in ('A', 'B', 'w_gate', 'wt_w', 'wt_b', 'wd_w', 'wd_b', 'scale')}
    del _L0_ffn_all

    def _L1_xattn_setup():
        import jax, jax.numpy as jnp
        import numpy as np
        HEADS = 8
        DIM_HEAD = 64
        DIM = 128
        CTX_DIM = 128
        HIDDEN = HEADS * DIM_HEAD
        key = jax.random.key(seed)
        ks = jax.random.split(key, 7)
        b, n, m = (2, 256, 256)
        x = jax.random.normal(ks[0], (b, n, DIM), dtype=jnp.float32)
        context = jax.random.normal(ks[1], (b, m, CTX_DIM), dtype=jnp.float32)
        Wq = jax.random.normal(ks[2], (DIM, HIDDEN), dtype=jnp.float32) * (1.0 / np.sqrt(DIM))
        Wk = jax.random.normal(ks[3], (CTX_DIM, HIDDEN), dtype=jnp.float32) * (1.0 / np.sqrt(CTX_DIM))
        Wv = jax.random.normal(ks[4], (CTX_DIM, HIDDEN), dtype=jnp.float32) * (1.0 / np.sqrt(CTX_DIM))
        Wo = jax.random.normal(ks[5], (HIDDEN, DIM), dtype=jnp.float32) * (1.0 / np.sqrt(HIDDEN))
        bo = jax.random.normal(ks[6], (DIM,), dtype=jnp.float32) * 0.01
        return {'x': x, 'context': context, 'Wq': Wq, 'Wk': Wk, 'Wv': Wv, 'Wo': Wo, 'bo': bo}
    _L1_xattn_all = _L1_xattn_setup()
    _L1_xattn_in = {k: v for k, v in _L1_xattn_all.items() if k in ('Wq', 'Wk', 'Wv', 'Wo', 'bo')}
    del _L1_xattn_all

    def _L1_ffn_setup():
        import jax, jax.numpy as jnp
        import numpy as np
        B, S, D, F, E, TOP_K = (4, 256, 128, 512, 8, 2)
        LN_EPS = 1e-05
        key = jax.random.key(seed)
        ks = jax.random.split(key, 4)
        sc = lambda fan_in: 1.0 / np.sqrt(fan_in)
        return {'x': jax.random.normal(ks[0], (B, S, D), jnp.float32), 'W1': jax.random.normal(ks[1], (E, D, F), jnp.float32) * sc(D), 'b1': jnp.zeros((E, F), jnp.float32), 'W2': jax.random.normal(ks[2], (E, F, D), jnp.float32) * sc(F), 'b2': jnp.zeros((E, D), jnp.float32), 'Wr': jax.random.normal(ks[3], (D, E), jnp.float32) * sc(D), 'br': jnp.zeros((E,), jnp.float32), 'gamma': jnp.ones((D,), jnp.float32), 'beta': jnp.zeros((D,), jnp.float32)}
    _L1_ffn_all = _L1_ffn_setup()
    _L1_ffn_in = {k: v for k, v in _L1_ffn_all.items() if k in ('W1', 'b1', 'W2', 'b2', 'Wr', 'br', 'gamma', 'beta')}
    del _L1_ffn_all
    return {'x': x, 'ctx_1024': ctx_1024, 'g_xattn': g_xattn, 'g_ffn': g_ffn, 'L0_xattn_W_q': _L0_xattn_in['W_q'], 'L0_xattn_W_k': _L0_xattn_in['W_k'], 'L0_xattn_W_v': _L0_xattn_in['W_v'], 'L0_xattn_b_v': _L0_xattn_in['b_v'], 'L0_xattn_W_o': _L0_xattn_in['W_o'], 'L0_xattn_b_o': _L0_xattn_in['b_o'], 'L0_ffn_A': _L0_ffn_in['A'], 'L0_ffn_B': _L0_ffn_in['B'], 'L0_ffn_w_gate': _L0_ffn_in['w_gate'], 'L0_ffn_wt_w': _L0_ffn_in['wt_w'], 'L0_ffn_wt_b': _L0_ffn_in['wt_b'], 'L0_ffn_wd_w': _L0_ffn_in['wd_w'], 'L0_ffn_wd_b': _L0_ffn_in['wd_b'], 'L0_ffn_scale': _L0_ffn_in['scale'], 'L1_xattn_Wq': _L1_xattn_in['Wq'], 'L1_xattn_Wk': _L1_xattn_in['Wk'], 'L1_xattn_Wv': _L1_xattn_in['Wv'], 'L1_xattn_Wo': _L1_xattn_in['Wo'], 'L1_xattn_bo': _L1_xattn_in['bo'], 'L1_ffn_W1': _L1_ffn_in['W1'], 'L1_ffn_b1': _L1_ffn_in['b1'], 'L1_ffn_W2': _L1_ffn_in['W2'], 'L1_ffn_b2': _L1_ffn_in['b2'], 'L1_ffn_Wr': _L1_ffn_in['Wr'], 'L1_ffn_br': _L1_ffn_in['br'], 'L1_ffn_gamma': _L1_ffn_in['gamma'], 'L1_ffn_beta': _L1_ffn_in['beta']}

def reference(x, ctx_1024, g_xattn, g_ffn, L0_xattn_W_q, L0_xattn_W_k, L0_xattn_W_v, L0_xattn_b_v, L0_xattn_W_o, L0_xattn_b_o, L0_ffn_A, L0_ffn_B, L0_ffn_w_gate, L0_ffn_wt_w, L0_ffn_wt_b, L0_ffn_wd_w, L0_ffn_wd_b, L0_ffn_scale, L1_xattn_Wq, L1_xattn_Wk, L1_xattn_Wv, L1_xattn_Wo, L1_xattn_bo, L1_ffn_W1, L1_ffn_b1, L1_ffn_W2, L1_ffn_b2, L1_ffn_Wr, L1_ffn_br, L1_ffn_gamma, L1_ffn_beta):
    import jax
    import jax.numpy as jnp

    def _L0_xattn_ref(q, k, v, W_q, W_k, W_v, b_v, W_o, b_o):
        import jax, jax.numpy as jnp
        import numpy as np
        E_PHI = 128
        E_F = 128
        HID = 128
        N_HEADS = 16
        HEAD_DIM = HID // N_HEADS
        B, S, _ = q.shape
        qh = (q @ W_q).reshape(B, S, N_HEADS, HEAD_DIM)
        kh = (k @ W_k).reshape(B, S, N_HEADS, HEAD_DIM)
        vh = (v @ W_v + b_v).reshape(B, S, N_HEADS, HEAD_DIM)
        scale = 1.0 / jnp.sqrt(jnp.float32(HEAD_DIM))
        scores = jnp.einsum('bihd,bjhd->bhij', qh, kh) * scale
        i = jnp.arange(S)[:, None]
        j = jnp.arange(S)[None, :]
        keep = (j < i) | (i == 0) & (j == 0)
        scores = jnp.where(keep, scores, jnp.float32(-jnp.inf))
        probs = jax.nn.softmax(scores, axis=-1)
        attn = jnp.einsum('bhij,bjhd->bihd', probs, vh).reshape(B, S, HID)
        return attn @ W_o + b_o

    def _L0_ffn_ref(feats, A, B, w_gate, wt_w, wt_b, wd_w, wd_b, scale):
        import jax, jax.numpy as jnp
        import numpy as np
        from jax import lax
        TOP_K = 1
        Bsz, N, C = feats.shape
        x = feats.reshape(-1, C)
        n = x.shape[0]
        logits = x @ w_gate
        top_vals, top_idx = lax.top_k(logits, TOP_K)
        top_g = jax.nn.softmax(top_vals, axis=-1)
        gates = jnp.zeros_like(logits).at[jnp.arange(n)[:, None], top_idx].set(top_g)
        tokens = jnp.einsum('elr,erc->elc', A, B)
        attn = jnp.einsum('nc,elc->nel', x, tokens) * C ** (-0.5)
        attn = jax.nn.softmax(attn, axis=-1)
        val = jnp.einsum('elc,dc->eld', tokens, wt_w) + wt_b
        delta_f = jnp.einsum('nel,eld->ned', attn[:, :, 1:], val[:, 1:, :])
        delta = (jnp.einsum('ned,cd->nec', delta_f + x[:, None, :], wd_w) + wd_b) * scale[0]
        combined = jnp.sum(jnp.exp(delta) * gates[:, :, None], axis=1)
        combined = jnp.where(combined == 0, jnp.finfo(jnp.float32).eps, combined)
        out = jnp.log(combined)
        return feats + out.reshape(Bsz, N, C)

    def _L1_xattn_ref(x, context, Wq, Wk, Wv, Wo, bo):
        import jax, jax.numpy as jnp
        import numpy as np
        HEADS = 8
        DIM_HEAD = 64
        DIM = 128
        CTX_DIM = 128
        HIDDEN = HEADS * DIM_HEAD
        b, n, _ = x.shape
        m = context.shape[1]
        scale = DIM_HEAD ** (-0.5)
        q = (x @ Wq).reshape(b, n, HEADS, DIM_HEAD).transpose(0, 2, 1, 3)
        k = (context @ Wk).reshape(b, m, HEADS, DIM_HEAD).transpose(0, 2, 1, 3)
        v = (context @ Wv).reshape(b, m, HEADS, DIM_HEAD).transpose(0, 2, 1, 3)
        scores = jnp.einsum('bhnd,bhmd->bhnm', q, k) * scale
        attn = jax.nn.softmax(scores, axis=-1)
        out = jnp.einsum('bhnm,bhmd->bhnd', attn, v)
        out = out.transpose(0, 2, 1, 3).reshape(b, n, HIDDEN)
        return out @ Wo + bo

    def _L1_ffn_ref(x, W1, b1, W2, b2, Wr, br, gamma, beta):
        import jax, jax.numpy as jnp
        import numpy as np
        B, S, D, F, E, TOP_K = (4, 256, 128, 512, 8, 2)
        LN_EPS = 1e-05
        b, s, d = x.shape
        e = Wr.shape[1]
        rw = jax.nn.softmax(x.mean(axis=1) @ Wr + br, axis=-1)
        x_flat = x.reshape(-1, d)
        rw_tok = jnp.repeat(rw, s, axis=0)
        tk_w, tk_i = jax.lax.top_k(rw_tok, TOP_K)
        tk_w = jax.nn.softmax(tk_w, axis=-1)
        h = jax.nn.gelu(jnp.einsum('nd,edf->enf', x_flat, W1) + b1[:, None, :], approximate=False)
        expert_out = jnp.einsum('enf,efd->end', h, W2) + b2[:, None, :]
        onehot = jax.nn.one_hot(tk_i, e, dtype=x.dtype)
        cw = jnp.einsum('nk,nke->ne', tk_w, onehot)
        out = jnp.einsum('ne,end->nd', cw, expert_out).reshape(b, s, d)
        y = out + x
        mu = y.mean(axis=-1, keepdims=True)
        var = y.var(axis=-1, keepdims=True)
        return (y - mu) / jnp.sqrt(var + LN_EPS) * gamma + beta
    x = x + jnp.tanh(g_xattn[0]) * _L0_xattn_ref(_layernorm(x, axis=-1), ctx_1024, ctx_1024, L0_xattn_W_q, L0_xattn_W_k, L0_xattn_W_v, L0_xattn_b_v, L0_xattn_W_o, L0_xattn_b_o)
    x = x + jnp.tanh(g_ffn[0]) * _L0_ffn_ref(_layernorm(x, axis=-1), L0_ffn_A, L0_ffn_B, L0_ffn_w_gate, L0_ffn_wt_w, L0_ffn_wt_b, L0_ffn_wd_w, L0_ffn_wd_b, L0_ffn_scale)
    x = x + jnp.tanh(g_xattn[1]) * _L1_xattn_ref(_layernorm(x, axis=-1), ctx_1024, L1_xattn_Wq, L1_xattn_Wk, L1_xattn_Wv, L1_xattn_Wo, L1_xattn_bo)
    x = x + jnp.tanh(g_ffn[1]) * _L1_ffn_ref(_layernorm(x, axis=-1), L1_ffn_W1, L1_ffn_b1, L1_ffn_W2, L1_ffn_b2, L1_ffn_Wr, L1_ffn_br, L1_ffn_gamma, L1_ffn_beta)
    return x

_drawn_inputs = setup_inputs


def setup_inputs(seed=0):
    import zlib

    import numpy as np

    out = dict(_drawn_inputs(seed))
    spreads = {'g_ffn': (-1.0, 0.2),
     'L1_ffn_b1': (0.0, 0.373),
     'L1_ffn_b2': (0.0, 0.1),
     'L1_ffn_br': (0.0, 0.692),
     'L1_ffn_gamma': (1.0, 0.2),
     'L1_ffn_beta': (0.0, 0.1)}
    factors = {'L0_xattn_W_q': 8.0,
     'L0_xattn_W_k': 8.0,
     'L0_xattn_W_v': 4.279,
     'L0_xattn_b_v': 22.964,
     'L0_xattn_b_o': 6.121,
     'L0_ffn_A': 47.906,
     'L0_ffn_B': 27.101,
     'L0_ffn_w_gate': 30.996,
     'L0_ffn_wt_w': 26.118,
     'L0_ffn_wt_b': 200.0,
     'L0_ffn_wd_w': 8.0,
     'L0_ffn_wd_b': 200.0,
     'L1_xattn_bo': 3.082}
    for name, (base, spread) in spreads.items():
        noise = np.random.default_rng([zlib.crc32(name.encode()), seed]).standard_normal(out[name].shape)
        drawn = base * np.exp(spread * noise) if base else spread * noise
        out[name] = jnp.asarray(drawn.astype(out[name].dtype))
    for name, factor in factors.items():
        out[name] = (out[name] * factor).astype(out[name].dtype)
    return out
```

```python
from contextlib import ExitStack

import concourse.bass as bass
from concourse import mybir

B, S, D = 4, 256, 128
P = 128
NT = B * S // P
H0, D0 = 16, 8
NX, NL, NR = 6, 100, 16
EL, ELT = 120, 5
H1, D1 = 8, 64
NE, F = 8, 512
FT = F // P
KR = 6 * D0
BIG = 1.0e30
EPS_LN = 1e-5
EPS_LOG = 1.1920928955078125e-07
V_G, V_BO0, V_BO1, V_WDB, V_GAM, V_BET, V_BR, V_SC = 0, 4, 132, 260, 388, 516, 644, 652
NVEC = 653
C_ID, C_MASK, C_L0, C_W6, C_IOTA = 0, 128, 384, 389, 395
NCONST = 403


def misc_uses():
    uses = []
    for b in range(B):
        uses += [("xT", 0, b)]
    for b in range(B):
        uses += [("mT", b)]
    for b in range(B):
        uses += [("oT", b), ("wo0", b), ("xT", 1, b)]
    for b in range(B):
        uses += [("xT", 2, b)]
    uses += [("q", 0, 0), ("q", 0, 1)]
    for n in range(4 * B):
        b, s = divmod(n, 4)
        uses += l1_events(b, s)
    for s in range(7):
        uses += l1_events(B, s)
    for b in range(B):
        uses += [("base", b)]
    return uses


def l1_events(b, s):
    ev = []
    if s == 1:
        ev = [("r2", b - 2)] if b >= 2 else []
        ev += [("q", b + 1, 0)] if b + 1 < B else []
    if s == 2:
        ev = [("r3", b - 2)] if b >= 2 else []
        ev += [("q", b + 1, 1)] if b + 1 < B else []
        ev += [("wo1", b - 1)] if b >= 1 else []
    if s == 3:
        ev = [("xT", 3, b - 1)] if b >= 1 else []
    if s == 0:
        ev = [("r1", b - 2)] if b >= 2 else []
    if s == 4:
        ev = [("r1", B - 1)]
    if s == 5:
        ev = [("r2", B - 1)]
    if s == 6:
        ev = [("r3", B - 1)]
    return ev


def build_program(nc, x, ctxT, w0, wo0, ab, wtd, wgate, vecs, cols, w1, wo1, wr, b12, w12, consts,
                  out, qk_scr, m_scr):
    fp32, bf16, u32 = mybir.dt.float32, mybir.dt.bfloat16, mybir.dt.uint32
    ALU = mybir.AluOpType
    ACT = mybir.ActivationFunctionType
    AXX = mybir.AxisListType.X
    MISC = {u: i for i, u in enumerate(misc_uses())}
    READ = {u: i + 1 for i, u in enumerate(
        [u for u in misc_uses() if u[0] in ("wo0", "wo1", "r1", "base")])}

    ctx = ExitStack()
    with ctx:
        def sb(name, shape, dt=fp32):
            return ctx.enter_context(nc.sbuf_tensor(name, shape, dt))

        def sem(name):
            return ctx.enter_context(nc.semaphore(name))

        W0 = sb("W0", [P, 3, P])
        WO0 = sb("WO0", [P, P])
        AB = sb("AB", [NR, NX * (NL + P)])
        WTD = sb("WTD", [P, 2, P])
        TG = sb("TG", [P, 606])
        VEC = sb("VEC", [P, NVEC])
        COL = sb("COL", [P, 2])
        W1 = sb("W1", [P, 3, F])
        WO1 = sb("WO1", [P, 4, P])
        WR = sb("WR", [P, NE])
        B12 = sb("B12", [NE, F + P])
        CST = sb("CST", [P, NCONST])
        ident = CST[:, C_ID:C_ID + P]
        IDB = sb("IDB", [P, P], bf16)
        MSKB = sb("MSKB", [P, 2, P], bf16)
        HALF = sb("HALF", [P, 2])
        TG4 = sb("TG4", [P, 4])
        GT = sb("GT", [P, P])
        X = sb("X", [P, NT, D])
        XH = sb("XH", [P, NT, D])
        XT = sb("XT", [P, B * S])
        CT = sb("CT", [P, B * S])
        ST = sb("ST", [P, NT, 6])
        MV = sb("MV", [P, NT, 2])
        VE = sb("VE", [P, NT])
        RS = sb("RS", [P, NT])
        QK = sb("QK", [P, 2, B, H0 * S], bf16)
        ONE = QK[64:66, 0, 0, :]
        QKh = QK[:, :, :, :].rearrange("p a b (h t) -> p a b h t", h=H0)
        BIGF = QK[:, :, :, :].rearrange("p a b n -> p (a b n)").bitcast(fp32)
        PARTS = sb("PARTS", [P, 2, 12, S], bf16)
        VA = sb("VA", [P, NT, H0, 32])
        PT0 = sb("PT0", [P, 3, 4, 384])
        VAF = VA[:, :, :, :].rearrange("p a b c -> p (a b c)")
        PT0F = PT0[:, :, :, :].rearrange("p a b c -> p (a b c)")
        PARTF = PARTS[:, :, :, :].rearrange("p a b c -> p (a b c)").bitcast(fp32)
        RES = PT0F[:, 2048:3072].rearrange("p (a n) -> p a n", a=2)
        MX0 = sb("MX0", [P, B, 2, H0])
        MP = sb("MP", [P, B, 2, 2, H0], bf16)
        MT = sb("MT", [32, 2, S], bf16)
        OTS = PARTF[:, 0:1024].rearrange("p (a n) -> p a n", a=2)
        RC0 = sb("RC0", [P, 2, 8])
        OD = sb("OD", [P, 2, 2, P])
        ODT = sb("ODT", [P, 2, S])
        VT = sb("VT", [P, NX * NL])
        VP = sb("VP", [EL, ELT, P])
        MX6 = sb("MX6", [P, 2, 6])
        GM = sb("GM", [P, 2])
        T1 = sb("T1", [P, 2, 6])
        T2 = sb("T2", [P, 2])
        NB6 = sb("NB6", [P, 2, 6])
        SH6 = sb("SH6", [P, 2, 6])
        TE = PARTF[:, 0:1200].rearrange("p (a n) -> p a n", a=2)
        SM0 = sb("SM0", [P, NT])
        RM0 = sb("RM0", [P, NT])
        PTE = VAF[0:EL, 2048:3328].rearrange("p (a t n) -> p a t n", a=2, t=ELT)
        XW = PARTF[:, 1200:1456].rearrange("p (a n) -> p a n", a=2)
        XWB = PARTF[:, 1456:1712].rearrange("p (a n) -> p a n", a=2)
        DL = PARTF[:, 1712:2224].rearrange("p (a n) -> p a n", a=2)
        WS = PARTF[:, 2224:2480]
        CE = VAF[:, 3328:3584]
        ZE = VAF[:, 3584:3840]
        LNV = VAF[:, 3840:4096]
        KT1 = sb("KT1", [P, 4, B * S])
        V1 = sb("V1", [P, NT, F])
        QT1 = VAF[:, 0:2048].rearrange("p (a c s) -> p a c s", a=2, c=4)
        OT1 = PT0F[:, 0:2048].rearrange("p (a c s) -> p a c s", a=2, c=4)
        PR = BIGF[:, 0:3072].rearrange("p (a h i j) -> p a h i j", a=3, h=2, i=2)
        PT1 = BIGF[:, 3072:6144].rearrange("p (a h j i) -> p a h j i", a=3, h=2, j=2)
        W12 = BIGF[:, 6144:14336].rearrange("p (m n) -> p m n", m=8)
        HT = BIGF[:, 14336:16384].rearrange("p (a f s) -> p a f s", a=2, f=FT)
        MX1 = sb("MX1", [P, 2, 4])
        NM1 = sb("NM1", [P, 2, 4])
        SM1 = sb("SM1", [P, 2, 4])
        RC1 = sb("RC1", [P, 2, 4])
        MS = sb("MS", [P, B])
        LG = sb("LG", [P, B, NE])
        MR = sb("MR", [P, B])
        ER = sb("ER", [P, B, NE])
        SR = sb("SR", [P, B])
        RR = sb("RR", [P, B])
        RW = sb("RW", [P, B, NE])
        TOP = sb("TOP", [P, B, 8])
        IDX = sb("IDX", [P, B, 8], u32)
        IDF = sb("IDF", [P, B, 8])
        DD = sb("DD", [P, B])
        E2 = sb("E2", [P, B])
        DEN = sb("DEN", [P, B])
        WK = sb("WK", [P, B, 2])
        OH = sb("OH", [P, B, 3, NE])
        OHT = sb("OHT", [NE, B, 3, P])
        B1S = sb("B1S", [P, B, FT, 2])
        Y = PARTF[:, 2480:2992].rearrange("p (a n) -> p a n", a=2)

        PS = ctx.enter_context(nc.psum_tensor("PS", [P, 8, 512], fp32))
        PSF = PS[:, :, :].rearrange("p k n -> p (k n)")

        def banks(k, n=512):
            return PSF[:, 512 * k:512 * k + n]

        misc = banks(7)

        d_x, d_c, d_ctx, d_w0, d_vec = map(sem, ("d_x", "d_c", "d_ctx", "d_w0", "d_vec"))
        d_w1, d_ab, d_late = map(sem, ("d_w1", "d_ab", "d_late"))
        s_cst, s_one, s_va0, s_tanh, s_gt = map(sem, ("s_cst", "s_one", "s_va0", "s_tanh", "s_gt"))
        s_xbo = sem("s_xbo")
        s_mv, s_rstd, s_xh, s_xt = map(sem, ("s_mv", "s_rstd", "s_xh", "s_xt"))
        s_mp7, s_mc7 = sem("s_misc_full"), sem("s_misc_free")
        s_qk, s_hi, s_res, s_parts, s_rep = map(sem, ("s_qk", "s_hi", "s_res", "s_parts", "s_rep"))
        s_v0p, s_v0 = sem("s_v0p"), sem("s_v0")
        d_scr, d_one = sem("d_scr"), sem("d_one")
        d_qk = [sem(f"d_qk_{b}") for b in range(B)]
        d_shift = [sem(f"d_shift_{b}") for b in range(B)]
        s_s0, s_mx0, s_mparts, s_mt = map(sem, ("s_s0", "s_mx0", "s_mparts", "s_mt"))
        d_mscr = sem("d_mscr")
        s_tok, s_tokc, s_vt, s_vtc, s_vp, s_vpc = map(sem, ("s_tok", "s_tokc", "s_vt", "s_vtc", "s_vp", "s_vpc"))
        s_k1, s_k1c = sem("s_k1"), sem("s_k1c")
        s_st, s_p0, s_pm, s_av0, s_ots, s_ott, s_od, s_odt = map(
            sem, ("s_st", "s_p0", "s_pm", "s_av0", "s_ots", "s_ott", "s_od", "s_odt"))
        s_lg, s_te, s_pe, s_pte, s_ptec, s_acc, s_xw, s_xwb, s_dl = map(
            sem, ("s_lg", "s_te", "s_pe", "s_pte", "s_ptec", "s_acc", "s_xw", "s_xwb", "s_dl"))
        s_ce, s_cg, s_ln, s_ws = map(sem, ("s_ce", "s_cg", "s_ln", "s_ws"))
        s_s1, s_nm1, s_e1, s_p1, s_t1, s_pt1a, s_pt1d, s_av1, s_ot1 = map(
            sem, ("s_s1", "s_nm1", "s_e1", "s_p1", "s_t1", "s_pt1a", "s_pt1d", "s_av1", "s_ot1"))
        s_q1, s_lgr, s_er, s_idx, s_dd, s_e2, s_oh, s_oht, s_b1s = map(
            sem, ("s_q1", "s_lgr", "s_er", "s_idx", "s_dd", "s_e2", "s_oh", "s_oht", "s_b1s"))
        d_w12 = [sem(f"d_w12_{b}") for b in range(B)]
        s_h, s_g, s_y, s_yc, s_fin, d_out = map(sem, ("s_h", "s_g", "s_y", "s_yc", "s_fin", "d_out"))
        c_dve, c_act, c_pool = sem("c_dve"), sem("c_act"), sem("c_pool")

        def chain(eng, s):
            count = [0]

            def link(ins):
                count[0] += 1
                ins.then_inc(s, 1)
                eng.wait_ge(s, count[0])
            return link

        block = ctx.enter_context(nc.Block())

        @block.sync
        def _(sp):
            sp.dma_start(X[:, :, :], x.rearrange("(t p) d -> p t d", p=P)).then_inc(d_x, 16)
            sp.dma_start(CT[:, :], ctxT).then_inc(d_ctx, 16)
            sp.dma_start(W0[:, :, :], w0).then_inc(d_w0, 16)
            sp.dma_start(COL[:, :], cols).then_inc(d_w0, 16)
            sp.dma_start(VEC[:, :], vecs.partition_broadcast(P)).then_inc(d_vec, 16)
            sp.dma_start(W1[:, :, :], w1).then_inc(d_w1, 16)
            sp.dma_start(AB[:, :], ab).then_inc(d_ab, 16)
            sp.dma_start(WTD[:, :, :], wtd).then_inc(d_ab, 16)
            sp.dma_start(TG[:, 300:306], wgate).then_inc(d_ab, 16)
            for b in range(B):
                sp.wait_ge(s_rep, b + 1)
                sp.dma_start(qk_scr[b].rearrange("a k p t -> p (a k) t"),
                             PARTS[:, b % 2]).then_inc(d_scr, 16)
                sp.wait_ge(d_scr, 16 * (b + 1))
                sp.dma_start(QK[0:KR, :, b, :],
                             qk_scr[b].rearrange("a k (r h) t -> (k r) a (h t)", h=H0)).then_inc(d_qk[b], 16)
            sp.wait_ge(s_one, 1)
            sp.dma_start(QK[KR:KR + 2, 1, :, :],
                         ONE.unsqueeze(1).to_broadcast([2, B, H0 * S])).then_inc(d_one, 16)
            sp.dma_start(WO0[:, :], wo0).then_inc(d_late, 16)
            sp.dma_start(WO1[:, :, :], wo1).then_inc(d_late, 16)
            sp.dma_start(WR[:, :], wr).then_inc(d_late, 16)
            sp.dma_start(B12[:, :], b12).then_inc(d_late, 16)
            for b in range(B):
                sp.wait_ge(s_mt, b + 1)
                sp.dma_start(m_scr[b], MT[:, b % 2, :]).then_inc(d_mscr, 16)
                sp.wait_ge(d_mscr, 16 * (b + 1))
                sp.dma_start(QK[KR:KR + 2, 0, b, :],
                             m_scr[b].rearrange("(k h) t -> k (h t)", k=2)).then_inc(d_shift[b], 16)
            for b in range(B):
                sp.wait_ge(s_idx, b + 1)
                for k in range(2):
                    e = sp.value_load(IDX[0:1, b, k:k + 1], min_val=0, max_val=NE - 1)
                    sp.dma_start(W12[:, 2 * b + k, :],
                                 w12[bass.ds(e, 1)].rearrange("o p n -> (o p) n")).then_inc(d_w12[b], 16)
            for b in range(B):
                sp.wait_ge(s_fin, b + 1)
                sp.dma_start(out[b * S:(b + 1) * S].rearrange("(t p) d -> p t d", p=P),
                             X[:, 2 * b:2 * b + 2, :]).then_inc(d_out, 16)
            sp.wait_ge(d_out, 16 * B)

        @block.gpsimd
        def _(pool):
            link = chain(pool, c_pool)
            g = nc.gpsimd
            g.memset(HALF[:, :], -0.5)
            g.memset(VA[:, :, :, :], 0.0).then_inc(s_va0, 1)
            pool.wait_ge(s_va0, 1)
            g.memset(VA[:, :, :, 8:9], 1.0).then_inc(s_va0, 1)

            def rstd(n):
                b = n % B
                pool.wait_ge(s_mv, n + 1)
                link(g.tensor_scalar_add(VE[:, 2 * b:2 * b + 2], MV[:, 2 * b:2 * b + 2, 1], EPS_LN))
                g.tensor_tensor(RS[:, 2 * b:2 * b + 2], VE[:, 2 * b:2 * b + 2], HALF[:, :],
                                ALU.pow).then_inc(s_rstd, 1)

            for b in range(B):
                rstd(b)
            for b in range(B):
                pool.wait_ge(s_parts, b + 1)
                pt = PARTS[:, b % 2]
                g.tensor_copy(pt[:, 3:6:2], pt[:, 0:1].to_broadcast([P, 2, S]))
                g.tensor_copy(pt[:, 4:5], pt[:, 1:2])
                g.tensor_copy(pt[:, 7:9], pt[:, 6:7].to_broadcast([P, 2, S]))
                g.tensor_copy(pt[:, 10:11], pt[:, 9:10]).then_inc(s_rep, 1)
            pool.wait_ge(s_rep, B)
            g.memset(ONE, 1.0).then_inc(s_one, 1)
            pool.wait_ge(s_one, 1)

            def add_bias(n, off, gate):
                b = n % B
                xs = X[:, 2 * b:2 * b + 2, :]
                g.tensor_tensor(xs, xs, VEC[:, off:off + D].unsqueeze(1).to_broadcast([P, 2, D]),
                                ALU.add).then_inc(s_xbo, 1)

            pool.wait_ge(d_vec, 16)
            pool.wait_ge(s_tanh, 1)
            for off, gate in ((V_BO0, 0), (V_BO1, 1), (V_BET, 3)):
                g.tensor_tensor(VEC[:, off:off + D], VEC[:, off:off + D],
                                TG4[:, gate:gate + 1].to_broadcast([P, D]), ALU.mult)
            link(g.tensor_tensor(GT[:, :], VEC[:, V_GAM:V_GAM + D],
                                 TG4[:, 3:4].to_broadcast([P, D]), ALU.mult))
            pool.wait_ge(s_xh, B)
            for b in range(B):
                add_bias(b, V_BO0, 0)
            for n in range(4 * B + 4):
                if n < 4 * B:
                    pool.wait_ge(s_p0, n + 1)
                    pt = PT0[:, n % 3]
                    g.affine_select(out=pt[:, :, 0:128], in_=pt[:, :, 0:128], compare_op=ALU.is_gt, fill=0.0,
                                    base=1, pattern=[[0, 4], [126, 128]], channel_multiplier=-127)
                    g.affine_select(out=pt[:, :, 256:384], in_=pt[:, :, 256:384], compare_op=ALU.is_gt,
                                    fill=0.0, base=0, pattern=[[0, 4], [1, 128]],
                                    channel_multiplier=-1).then_inc(s_pm, 1)
                if n >= 6 and n % 4 == 2:
                    rstd(B + n // 4 - 1)
            def tail(b):
                pool.wait_ge(s_ln, b + 1)
                g.tensor_tensor(WS, XH[:, 2 * b:2 * b + 2, :].rearrange("p t d -> p (t d)"), LNV,
                                ALU.add).then_inc(s_ws, 1)
                rstd(2 * B + b)
                pool.wait_ge(s_xh, 2 * B + b + 1)
                add_bias(B + b, V_BO1, 1)

            for n in range(NT):
                if n >= 3 and n % 2 == 1:
                    tail(n // 2 - 1)
                pool.wait_ge(s_xw, n + 1)
                if n >= 2:
                    pool.wait_ge(s_dl, n - 1)
                g.tensor_tensor(XWB[:, n % 2], XW[:, n % 2], VEC[:, V_WDB:V_WDB + D], ALU.add).then_inc(s_xwb, 1)
            tail(B - 1)
            for b in range(B):
                rstd(3 * B + b)
                pool.wait_ge(s_xh, 3 * B + b + 1)
                add_bias(2 * B + b, V_BET, 3)
            for b in range(B):
                rstd(4 * B + b)

        @block.scalar
        def _(act):
            a = nc.scalar
            link = chain(act, c_act)
            act.dma_start(CST[:, :], consts).then_inc(d_c, 16)

            def wait_misc(*use):
                act.wait_ge(s_mp7, MISC[use] + 1)

            def copy_xT(layer, b):
                wait_misc("xT", layer, b)
                kw = {"accum_out": MS[:, b:b + 1]} if layer == 3 else {}
                a.activation(XT[:, b * S:(b + 1) * S], misc[:, 0:S], ACT.Identity, **kw).then_inc(s_xt, 1)

            act.wait_ge(d_vec, 16)
            a.activation(TG4[:, :], VEC[:, V_G:V_G + 4], ACT.Tanh).then_inc(s_tanh, 1)
            act.wait_ge(d_c, 16)
            a.activation(IDB[:, :], ident, ACT.Copy)
            a.activation(MSKB[:, :, :], CST[:, C_MASK:C_MASK + 2 * P].rearrange("p (a b) -> p a b", a=2),
                         ACT.Copy).then_inc(s_cst, 1)
            act.wait_ge(s_va0, 2)
            for b in range(B):
                copy_xT(0, b)
                act.wait_ge(s_qk, b + 1)
                if b >= 2:
                    act.wait_ge(d_scr, 16 * (b - 1))
                a.activation(PARTS[:, b % 2, 0:7:6], banks(4 + b % 2).rearrange("p (a t) -> p a t", a=2),
                             ACT.Copy).then_inc(s_hi, 1)
                act.wait_ge(s_v0p, b + 1)
                a.activation(VA[:, 2 * b:2 * b + 2, :, 0:8],
                             banks(6, 256).rearrange("p (t h d) -> p t h d", t=2, h=H0),
                             ACT.Copy).then_inc(s_v0, 1)
            act.wait_ge(s_tok, 1)
            a.activation(TG[:, 0:300], banks(4, 300), ACT.Copy)
            a.activation(TG[:, 306:606], banks(5, 300), ACT.Copy).then_inc(s_tokc, 1)
            act.wait_ge(s_vt, 1)
            act.wait_ge(d_w0, 32)
            a.activation(VT[:, 0:300], banks(4, 300), ACT.Identity, bias=COL[:, 1:2])
            a.activation(VT[:, 300:600], banks(5, 300), ACT.Identity, bias=COL[:, 1:2]).then_inc(s_vtc, 1)
            act.wait_ge(s_vp, 1)
            for t in range(ELT):
                a.activation(VP[:, t, :], banks(4, 640)[0:EL, t * P:(t + 1) * P], ACT.Copy,
                             scale=CST[0:EL, C_L0 + t:C_L0 + t + 1]).then_inc(s_vpc, 1)

            def kv(m):
                act.wait_ge(s_k1, m + 1)
                b, j = divmod(m, 4)
                src = banks(4 + m % 3)
                if j < 2:
                    dst = KT1[:, 2 * j:2 * j + 2, b * S:(b + 1) * S]
                    src = src.rearrange("p (c t) -> p c t", c=2)
                else:
                    dst = V1[:, 2 * b + j - 2, :]
                a.activation(dst, src, ACT.Copy).then_inc(s_k1c, 1)

            for b in range(B):
                for j in range(4):
                    kv(4 * b + j)
                wait_misc("mT", b)
                if b >= 2:
                    act.wait_ge(d_mscr, 16 * (b - 1))
                a.activation(MT[:, b % 2, :], misc[0:32, 0:128].bitcast(bf16), ACT.Copy).then_inc(s_mt, 1)

            for n in range(4 * B + 4):
                if n < 4 * B:
                    if n >= 3:
                        act.wait_ge(s_av0, n - 2)
                    act.wait_ge(s_st, n + 1)
                    a.activation(PT0[:, n % 3, :, 0:256],
                                 banks(2 * (n % 2), 1024).rearrange("p (h i) -> p h i", h=4),
                                 ACT.Exp, scale=D0 ** -0.5)
                    a.activation(PT0[:, n % 3, :, 256:384],
                                 banks(4).rearrange("p (h i) -> p h i", h=4),
                                 ACT.Exp, scale=D0 ** -0.5).then_inc(s_p0, 1)
                if n >= 6 and n % 4 == 2:
                    b = n // 4 - 1
                    wait_misc("oT", b)
                    a.activation(ODT[:, b % 2, :], misc[:, 0:S], ACT.Identity, bias=COL[:, 0:1]).then_inc(s_odt, 1)
                if n >= 7 and n % 4 == 3:
                    copy_xT(1, n // 4 - 1)

            def tail(b):
                act.wait_ge(s_dl, 2 * b + 2)
                a.activation(CE[:, :], DL[:, b % 2, :], ACT.Exp, scale=VEC[:, V_SC:V_SC + 1]).then_inc(s_ce, 1)
                act.wait_ge(s_cg, b + 1)
                if b >= 1:
                    act.wait_ge(s_ws, b)
                a.activation(LNV[:, :], CE[:, :], ACT.Ln).then_inc(s_ln, 1)

            for n in range(NT + 4):
                if n < NT:
                    act.wait_ge(s_te, n + 1)
                    a.activation(TE[:, n % 2, :], TE[:, n % 2, :], ACT.Exp, scale=D ** -0.5,
                                 accum_out=SM0[:, n:n + 1]).then_inc(s_pe, 1)
                if 1 <= n <= NT:
                    m = n - 1
                    act.wait_ge(s_pte, m + 1)
                    a.activation(PTE[:, m % 2].rearrange("p t n -> p (t n)"), banks(4, 640)[0:EL, :],
                                 ACT.Copy).then_inc(s_ptec, 1)
                    act.wait_ge(s_acc, m + 1)
                    if m >= 2:
                        act.wait_ge(s_xwb, m - 1)
                    a.activation(XW[:, m % 2], banks(6)[:, 128:256], ACT.Copy).then_inc(s_xw, 1)
                if n >= 3 and n % 2 == 1 and n // 2 - 1 < B:
                    tail(n // 2 - 1)
                if n >= 4 and n % 2 == 0 and n // 2 - 2 < B:
                    copy_xT(2, n // 2 - 2)

            def l1_event(ev):
                if ev[0] == "q":
                    _, b, j = ev
                    wait_misc("q", b, j)
                    a.activation(QT1[:, b % 2, 2 * j:2 * j + 2, :],
                                 misc.rearrange("p (c t) -> p c t", c=2), ACT.Copy).then_inc(s_q1, 1)
                if ev[0] == "xT":
                    copy_xT(ev[1], ev[2])
                if ev[0] == "r1":
                    b = ev[1]
                    act.wait_ge(s_lgr, b + 1)
                    a.activation(ER[:, b, :], LG[:, b, :], ACT.Exp, bias=MR[:, b:b + 1],
                                 accum_out=SR[:, b:b + 1]).then_inc(s_er, 1)
                    act.wait_ge(s_dd, b + 1)
                    a.activation(E2[:, b:b + 1], DD[:, b:b + 1], ACT.Exp).then_inc(s_e2, 1)

            for j in range(2):
                l1_event(("q", 0, j))
            for n in range(4 * B + 2):
                b, s = divmod(n, 4)
                if 1 <= n <= 4 * B:
                    act.wait_ge(s_t1, n)
                    a.activation(PT1[:, (n - 1) % 3, 1].rearrange("p j i -> p (j i)"), banks(5),
                                 ACT.Copy).then_inc(s_pt1a, 1)
                if n < 4 * B:
                    act.wait_ge(s_nm1, n + 1)
                    for h in range(2):
                        for it in range(2):
                            last = a.activation(PR[:, n % 3, h, it, :],
                                                banks(2 * (n % 2) + h)[:, it * S:(it + 1) * S], ACT.Exp,
                                                scale=D1 ** -0.5, bias=NM1[:, n % 2, 2 * h + it:2 * h + it + 1],
                                                accum_out=SM1[:, n % 2, 2 * h + it:2 * h + it + 1])
                    last.then_inc(s_e1, 1)
                if n >= 2 and n % 2 == 1:
                    p = (n - 3) // 2
                    act.wait_ge(s_av1, 2 * p + 2)
                    a.activation(OT1[:, (p // 2) % 2, 2 * (p % 2):2 * (p % 2) + 2, :],
                                 banks(6).rearrange("p (c t) -> p c t", c=2), ACT.Copy).then_inc(s_ot1, 1)
                if n < 4 * B:
                    for ev in l1_events(b, s):
                        l1_event(ev)
            for s in range(7):
                for ev in l1_events(B, s):
                    l1_event(ev)

            for m in range(2 * B):
                act.wait_ge(s_b1s, m // 2 + 1)
                act.wait_ge(s_h, m + 1)
                if m >= 2:
                    act.wait_ge(s_y, m - 1)
                for f in range(FT):
                    last = a.activation(HT[:, m % 2, f, :], banks(2 * (m % 2), 1024)[:, f * S:(f + 1) * S],
                                        ACT.Gelu, bias=B1S[:, m // 2, f, m % 2:m % 2 + 1])
                last.then_inc(s_g, 1)

        @block.vector
        def _(dve):
            v = nc.vector
            link = chain(dve, c_dve)

            def wait_misc(*use):
                dve.wait_ge(s_mp7, MISC[use] + 1)

            def norm(layer, b):
                for t in (2 * b, 2 * b + 1):
                    last = v.bn_stats(ST[:, t, :], X[:, t, :])
                link(last)
                for t in (2 * b, 2 * b + 1):
                    last = v.bn_aggr(MV[:, t, :], ST[:, t, :])
                last.then_inc(s_mv, 1)
                dve.wait_ge(s_rstd, B * layer + b + 1)
                for t in (2 * b, 2 * b + 1):
                    last = v.tensor_scalar(XH[:, t, :], X[:, t, :], MV[:, t, 0:1], RS[:, t:t + 1],
                                           ALU.subtract, ALU.mult)
                last.then_inc(s_xh, 1)

            dve.wait_ge(d_x, 16)
            for b in range(B):
                norm(0, b)
            for b in range(B):
                dve.wait_ge(s_hi, b + 1)
                ps = banks(4 + b % 2).rearrange("p (a t) -> p a t", a=2)
                res = RES[:, b % 2, :].rearrange("p (a t) -> p a t", a=2)
                pt = PARTS[:, b % 2]
                v.tensor_tensor(res, ps, pt[:, 0:7:6], ALU.subtract).then_inc(s_res, 1)
                dve.wait_ge(s_res, b + 1)
                link(v.tensor_copy(pt[:, 1:10:8], res))
                v.tensor_tensor(pt[:, 2:12:9], res, pt[:, 1:10:8], ALU.subtract).then_inc(s_parts, 1)

            for b in range(B):
                for u in range(6):
                    n = 6 * b + u
                    dve.wait_ge(s_s0, n + 1)
                    if u < 4:
                        dst, w = MX0[:, b, 1, 4 * u:4 * u + 4], S
                    else:
                        dst, w = MX0[:, b, 0, 8 * (u - 4):8 * (u - 4) + 8], P
                    v.tensor_reduce(dst, banks(2 * (n % 2), 1024).rearrange("p (h j) -> p h j", j=w),
                                    AXX, ALU.max, negate=True).then_inc(s_mx0, 1)
                dve.wait_ge(s_mx0, 6 * b + 6)
                link(v.tensor_copy(MP[:, b, :, 0, :], MX0[:, b]))
                v.tensor_tensor(MP[:, b, :, 1, :], MX0[:, b], MP[:, b, :, 0, :], ALU.subtract).then_inc(s_mparts, 1)

            def heads_out(pp):
                dve.wait_ge(s_av0, 2 * pp + 2)
                v.tensor_copy(OTS[:, pp % 2, :], banks(5)).then_inc(s_ots, 1)

            def heads_norm(pp):
                b, half = divmod(pp, 2)
                dve.wait_ge(s_ott, pp + 1)
                z = banks(6).rearrange("p (i h c) -> p i h c", i=2, h=8)
                link(v.reciprocal(RC0[:, :, :], z[:, :, :, 8]))
                v.tensor_tensor(OD[:, b % 2, :, 64 * half:64 * half + 64].rearrange("p i (h d) -> p i h d", h=8),
                                z[:, :, :, 0:8], RC0[:, :, :].unsqueeze(3).to_broadcast([P, 2, 8, 8]),
                                ALU.mult).then_inc(s_od, 1)

            def add_wo(use, b, gate, off, nbias):
                wait_misc(use, b)
                dve.wait_ge(s_xbo, nbias)
                xs = X[:, 2 * b:2 * b + 2, :].rearrange("p t d -> p (t d)")
                ins = v.scalar_tensor_tensor(xs, misc[:, off:off + S], TG4[:, gate:gate + 1], xs, ALU.mult, ALU.add)
                ins.then_inc(s_mc7, 1)
                dve.wait_ge(s_mc7, READ[(use, b)])

            for n in range(4 * B + 4):
                if n >= 2 and n % 2 == 0 and (n - 2) // 2 < 2 * B:
                    heads_out((n - 2) // 2)
                if n >= 3 and n % 2 == 1 and (n - 3) // 2 < 2 * B:
                    heads_norm((n - 3) // 2)
                if n >= 6 and n % 4 == 2:
                    b = n // 4 - 1
                    add_wo("wo0", b, 0, S, b + 1)
                    norm(1, b)

            def finish_tile(n):
                dve.wait_ge(s_acc, n + 1)
                link(v.reciprocal(RM0[:, n:n + 1], SM0[:, n:n + 1]))
                dve.wait_ge(s_xwb, n + 1)
                if n >= 4:
                    dve.wait_ge(s_ce, n // 2 - 1)
                v.scalar_tensor_tensor(DL[:, (n // 2) % 2, (n % 2) * D:(n % 2 + 1) * D], banks(6)[:, 0:D],
                                       RM0[:, n:n + 1], XWB[:, n % 2], ALU.mult, ALU.add).then_inc(s_dl, 1)

            def guard(b):
                dve.wait_ge(s_ce, b + 1)
                link(v.tensor_scalar(ZE[:, :], CE[:, :], 0.0, EPS_LOG, ALU.is_equal, ALU.mult))
                v.tensor_tensor(CE[:, :], CE[:, :], ZE[:, :], ALU.add).then_inc(s_cg, 1)

            def close0(b):
                dve.wait_ge(s_ws, b + 1)
                xs = X[:, 2 * b:2 * b + 2, :].rearrange("p t d -> p (t d)")
                link(v.scalar_tensor_tensor(xs, WS[:, :], TG4[:, 2:3], xs, ALU.mult, ALU.add))
                norm(2, b)

            for n in range(NT + 4):
                if n < NT:
                    k = n % 2
                    dve.wait_ge(s_lg, n + 1)
                    lg = banks(2 * k, 1024).rearrange("p (a c) -> p a c", a=2)[:, :, 0:300].rearrange(
                        "p a (e l) -> p a e l", e=3)
                    gate = banks(2 * k)[:, 300:306]
                    v.tensor_reduce(MX6[:, k, :], lg, AXX, ALU.max)
                    link(v.tensor_reduce(GM[:, k:k + 1], gate, AXX, ALU.max))
                    link(v.scalar_tensor_tensor(T1[:, k, :], gate, GM[:, k:k + 1], CST[:, C_W6:C_W6 + 6],
                                                ALU.is_ge, ALU.mult))
                    link(v.tensor_reduce(T2[:, k:k + 1], T1[:, k, :], AXX, ALU.max))
                    link(v.tensor_scalar(NB6[:, k, :], T1[:, k, :], T2[:, k:k + 1], BIG, ALU.is_lt, ALU.mult))
                    link(v.tensor_tensor(SH6[:, k, :], MX6[:, k, :], NB6[:, k, :], ALU.add))
                    if n >= 2:
                        dve.wait_ge(s_pte, n - 1)
                    v.tensor_tensor(TE[:, k, :].rearrange("p (a e l) -> p a e l", a=2, e=3), lg,
                                    SH6[:, k, :].rearrange("p (a e) -> p a e", a=2).unsqueeze(3).to_broadcast(
                                        [P, 2, 3, NL]), ALU.subtract).then_inc(s_te, 1)
                if 1 <= n <= NT:
                    finish_tile(n - 1)
                if n >= 3 and n % 2 == 1 and n // 2 - 1 < B:
                    b = n // 2 - 1
                    guard(b)
                    close0(b)

            def route(b):
                wait_misc("r1", b)
                v.scalar_tensor_tensor(LG[:, b, :], misc[:, 0:NE], 1.0 / S, VEC[:, V_BR:V_BR + NE],
                                       ALU.mult, ALU.add).then_inc(s_mc7, 1)
                dve.wait_ge(s_mc7, READ[("r1", b)])
                v.tensor_reduce(MR[:, b:b + 1], LG[:, b, :], AXX, ALU.max, negate=True).then_inc(s_lgr, 1)
                dve.wait_ge(s_er, b + 1)
                link(v.reciprocal(RR[:, b:b + 1], SR[:, b:b + 1]))
                link(v.tensor_scalar(RW[:, b, :], ER[:, b, :], RR[:, b:b + 1], None, ALU.mult))
                link(v.max(TOP[:, b, :], RW[:, b, :]))
                v.tensor_tensor(DD[:, b:b + 1], TOP[:, b, 1:2], TOP[:, b, 0:1], ALU.subtract).then_inc(s_dd, 1)
                v.max_index(IDX[:, b, :], TOP[:, b, :], RW[:, b, :]).then_inc(s_idx, 1)
                dve.wait_ge(s_idx, b + 1)
                link(v.tensor_copy(IDF[:, b, :], IDX[:, b, :]))
                for k in range(2):
                    last = v.tensor_scalar(OH[:, b, k, :], CST[:, C_IOTA:C_IOTA + NE], IDF[:, b, k:k + 1], None,
                                           ALU.is_equal)
                dve.wait_ge(s_e2, b + 1)
                link(v.tensor_scalar(DEN[:, b:b + 1], E2[:, b:b + 1], 1.0, None, ALU.add))
                link(v.reciprocal(WK[:, b, 0:1], DEN[:, b:b + 1]))
                link(v.tensor_tensor(WK[:, b, 1:2], E2[:, b:b + 1], WK[:, b, 0:1], ALU.mult))
                link(v.tensor_scalar(OH[:, b, 2, :], OH[:, b, 0, :], WK[:, b, 0:1], None, ALU.mult))
                v.scalar_tensor_tensor(OH[:, b, 2, :], OH[:, b, 1, :], WK[:, b, 1:2], OH[:, b, 2, :],
                                       ALU.mult, ALU.add).then_inc(s_oh, 1)

            def l1_event(ev):
                if ev[0] == "wo1":
                    b = ev[1]
                    add_wo("wo1", b, 1, 0, B + b + 1)
                    norm(3, b)
                if ev[0] == "r1":
                    route(ev[1])
                if ev[0] == "r2":
                    b = ev[1]
                    wait_misc("r2", b)
                    v.tensor_copy(OHT[:, b].rearrange("e k p -> e (k p)"), misc[0:NE, 0:3 * P]).then_inc(s_oht, 1)
                if ev[0] == "r3":
                    b = ev[1]
                    wait_misc("r3", b)
                    v.tensor_copy(B1S[:, b].rearrange("p f k -> p (f k)"), misc[:, 0:2 * FT]).then_inc(s_b1s, 1)

            for n in range(4 * B + 1):
                b, s = divmod(n, 4)
                k = n % 2
                if n < 4 * B:
                    dve.wait_ge(s_s1, n + 1)
                    link(v.tensor_reduce(MX1[:, k, :], banks(2 * k, 1024).rearrange("p (c j) -> p c j", j=S),
                                         AXX, ALU.max, negate=True))
                    v.tensor_scalar(NM1[:, k, :], MX1[:, k, :], D1 ** -0.5, None, ALU.mult).then_inc(s_nm1, 1)
                if n >= 1:
                    dve.wait_ge(s_t1, n)
                    v.tensor_copy(PT1[:, (n - 1) % 3, 0].rearrange("p j i -> p (j i)"), banks(4)).then_inc(s_pt1d, 1)
                if n < 4 * B:
                    dve.wait_ge(s_e1, n + 1)
                    link(v.reciprocal(RC1[:, k, :], SM1[:, k, :]))
                    for h in range(2):
                        for it in range(2):
                            pr = PR[:, n % 3, h, it, :]
                            last = v.tensor_scalar(pr, pr, RC1[:, k, 2 * h + it:2 * h + it + 1], None, ALU.mult)
                    last.then_inc(s_p1, 1)
                    for ev in l1_events(b, s):
                        l1_event(ev)
            for s in range(7):
                for ev in l1_events(B, s):
                    l1_event(ev)

            for b in range(B):
                wait_misc("base", b)
                yb = Y[:, b % 2, :]
                v.tensor_tensor(yb, misc[:, 0:S], XH[:, 2 * b:2 * b + 2, :].rearrange("p t d -> p (t d)"),
                                ALU.add).then_inc(s_mc7, 1)
                dve.wait_ge(s_mc7, READ[("base", b)])
                dve.wait_ge(s_y, 2 * b + 2)
                ps = banks(4 + b % 2)
                link(v.scalar_tensor_tensor(yb, ps[:, 0:S], WK[:, b, 0:1], yb, ALU.mult, ALU.add))
                v.scalar_tensor_tensor(yb, ps[:, S:2 * S], WK[:, b, 1:2], yb, ALU.mult, ALU.add).then_inc(s_yc, 1)
                dve.wait_ge(s_yc, b + 1)
                for t in range(2):
                    last = v.bn_stats(ST[:, 2 * b + t, :], yb[:, t * D:(t + 1) * D])
                link(last)
                for t in (2 * b, 2 * b + 1):
                    last = v.bn_aggr(MV[:, t, :], ST[:, t, :])
                last.then_inc(s_mv, 1)
                dve.wait_ge(s_rstd, 4 * B + b + 1)
                for t in range(2):
                    last = v.tensor_scalar(yb[:, t * D:(t + 1) * D], yb[:, t * D:(t + 1) * D],
                                           MV[:, 2 * b + t, 0:1], RS[:, 2 * b + t:2 * b + t + 1],
                                           ALU.subtract, ALU.mult)
                link(last)
                y3 = yb.rearrange("p (t d) -> p t d", t=2)
                link(v.tensor_tensor(y3, y3, GT[:, :].unsqueeze(1).to_broadcast([P, 2, D]), ALU.mult))
                dve.wait_ge(s_xbo, 2 * B + b + 1)
                xs = X[:, 2 * b:2 * b + 2, :]
                v.tensor_tensor(xs, y3, xs, ALU.add).then_inc(s_fin, 1)

        @block.tensor
        def _(pe):
            mm = nc.tensor.matmul

            def take_misc(*use):
                i = MISC[use]
                if i:
                    prev = ORDER[i - 1]
                    s, c = READER[prev]
                    pe.wait_ge(s, c)

            ORDER = misc_uses()
            READER = {}
            nq = nxt = 0
            for u in ORDER:
                kind = u[0]
                if kind == "xT":
                    READER[u] = (s_xt, B * u[1] + u[2] + 1)
                elif kind == "mT":
                    READER[u] = (s_mt, u[1] + 1)
                elif kind == "oT":
                    READER[u] = (s_odt, u[1] + 1)
                elif kind == "q":
                    READER[u] = (s_q1, 2 * u[1] + u[2] + 1)
                elif kind == "r2":
                    READER[u] = (s_oht, u[1] + 1)
                elif kind == "r3":
                    READER[u] = (s_b1s, u[1] + 1)
                else:
                    READER[u] = (s_mc7, READ[u])

            def transpose_x(layer, b):
                take_misc("xT", layer, b)
                pe.wait_ge(s_xh, B * layer + b + 1)
                for t in range(2):
                    last = nc.tensor.transpose(misc[:, t * P:(t + 1) * P], XH[:, 2 * b + t, :], ident)
                last.then_inc(s_mp7, 1)

            pe.wait_ge(d_c, 16)
            for b in range(B):
                transpose_x(0, b)
                cols = slice(b * S, (b + 1) * S)
                if b == 0:
                    pe.wait_ge(d_w0, 32)
                    pe.wait_ge(d_ctx, 16)
                if b >= 2:
                    pe.wait_ge(s_parts, b - 1)
                bank = banks(4 + b % 2)
                mm(bank[:, S:2 * S], W0[:, 1, :], CT[:, cols], start=True, stop=True)
                pe.wait_ge(s_xt, b + 1)
                mm(bank[:, 0:S], W0[:, 0, :], XT[:, cols], start=True, stop=True).then_inc(s_qk, 1)
                if b >= 1:
                    pe.wait_ge(s_v0, b)
                for t in range(2):
                    last = mm(banks(6)[:, t * P:(t + 1) * P], CT[:, b * S + t * P:b * S + (t + 1) * P],
                              W0[:, 2, :], start=True, stop=True)
                last.then_inc(s_v0p, 1)

            pe.wait_ge(d_ab, 48)
            pe.wait_ge(s_parts, B)
            for e in range(NX):
                last = mm(banks(4 + e // 3)[:, (e % 3) * NL:(e % 3 + 1) * NL],
                          AB[:, NX * NL + e * P:NX * NL + (e + 1) * P], AB[:, e * NL:(e + 1) * NL],
                          start=True, stop=True)
            last.then_inc(s_tok, 1)
            pe.wait_ge(s_tokc, 1)
            for a in range(2):
                last = mm(banks(4 + a)[:, 0:300], WTD[:, 0, :], TG[:, 306 * a:306 * a + 300], start=True, stop=True)
            last.then_inc(s_vt, 1)
            pe.wait_ge(s_vtc, 1)
            for t in range(ELT):
                last = mm(banks(4, 640)[0:EL, t * P:(t + 1) * P], VT[:, t * EL:(t + 1) * EL], WTD[:, 1, :],
                          start=True, stop=True)
            last.then_inc(s_vp, 1)

            def kv(m):
                b, j = divmod(m, 4)
                if m == 0:
                    pe.wait_ge(d_w1, 16)
                    pe.wait_ge(s_v0, B)
                    pe.wait_ge(s_vpc, ELT)
                if m >= 3:
                    pe.wait_ge(s_k1c, m - 2)
                bank = banks(4 + m % 3)
                if j < 2:
                    for c in range(2):
                        last = mm(bank[:, c * S:(c + 1) * S], W1[:, 1, (2 * j + c) * P:(2 * j + c + 1) * P],
                                  CT[:, b * S:(b + 1) * S], start=True, stop=True)
                else:
                    t = 2 * b + j - 2
                    last = mm(bank, CT[:, t * P:(t + 1) * P], W1[:, 2, :], start=True, stop=True)
                last.then_inc(s_k1, 1)

            def scores0(b, u):
                n = 6 * b + u
                if n >= 2:
                    pe.wait_ge(s_mx0, n - 1)
                for c in range(2):
                    bank = banks(2 * (n % 2) + c)
                    if u < 4:
                        view = bank.rearrange("p (h j) -> p h j", h=2)
                        mm(view[:, :, P:2 * P], IDB[:, :], MSKB[:, 1:2, :].to_broadcast([P, 2, P]),
                           start=True, stop=False, skip_group_check=True)
                        for g in range(2):
                            h = 4 * u + 2 * c + g
                            last = mm(view[:, g, :], QKh[0:KR, 0, b, h, P:2 * P], QKh[0:KR, 1, b, h, :],
                                      start=False, stop=True, skip_group_check=True)
                    else:
                        view = bank.rearrange("p (h j) -> p h j", h=4)
                        mm(view, IDB[:, :], MSKB[:, 0:1, :].to_broadcast([P, 4, P]),
                           start=True, stop=False, skip_group_check=True)
                        for g in range(4):
                            h = 8 * (u - 4) + 4 * c + g
                            last = mm(view[:, g, :], QKh[0:KR, 0, b, h, 0:P], QKh[0:KR, 1, b, h, 0:P],
                                      start=False, stop=True, skip_group_check=True)
                last.then_inc(s_s0, 1)

            def transpose_max(b):
                take_misc("mT", b)
                pe.wait_ge(s_mparts, b + 1)
                out16 = misc[0:32, 0:128].bitcast(bf16)
                for it in range(2):
                    last = nc.tensor.transpose(out16[:, it * P:(it + 1) * P],
                                               MP[:, b, it].rearrange("p k h -> p (k h)"), IDB[:, :])
                last.then_inc(s_mp7, 1)

            pe.wait_ge(s_cst, 1)
            for b in range(B):
                kv(4 * b)
                kv(4 * b + 1)
                pe.wait_ge(d_qk[b], 16)
                for u in range(6):
                    scores0(b, u)
                    if u in (1, 3):
                        kv(4 * b + 2 + u // 2)
                transpose_max(b)

            def scores0T(n):
                b, hg = divmod(n, 4)
                if hg == 0:
                    pe.wait_ge(d_shift[b], 16)
                if n == 0:
                    pe.wait_ge(d_one, 16)
                    pe.wait_ge(s_k1c, 4 * B)
                if n < 2:
                    pe.wait_ge(s_mx0, 6 * B)
                else:
                    pe.wait_ge(s_p0, n - 1)
                for g in range(4):
                    h = 4 * hg + g
                    mm(banks(2 * (n % 2), 1024)[:, g * S:(g + 1) * S], QKh[0:KR + 2, 1, b, h, 0:P],
                       QKh[0:KR + 2, 0, b, h, :], start=True, stop=True)
                if n >= 1:
                    pe.wait_ge(s_p0, n)
                for g in range(4):
                    h = 4 * hg + g
                    last = mm(banks(4)[:, g * P:(g + 1) * P], QKh[0:KR + 2, 1, b, h, P:2 * P],
                              QKh[0:KR + 2, 0, b, h, P:2 * P], start=True, stop=True)
                last.then_inc(s_st, 1)

            def outputs0(n):
                b, hg = divmod(n, 4)
                if n == 0:
                    pe.wait_ge(s_v0, B)
                pe.wait_ge(s_pm, n + 1)
                if n >= 2 and n % 2 == 0:
                    pe.wait_ge(s_ots, n // 2)
                half = n % 2 * S
                for jt in range(2):
                    for g in range(4):
                        rows = slice(32 * g, 32 * g + 32)
                        src = PT0[:, n % 3, g, 0:256] if jt == 0 else PT0[:, n % 3, g, 256:384]
                        last = mm(banks(5)[rows, half + jt * P:half + S], VA[:, 2 * b + jt, 4 * hg + g, :], src,
                                  start=(jt == 0), stop=(jt == 1), skip_group_check=True)
                last.then_inc(s_av0, 1)

            def transpose_heads(pp):
                pe.wait_ge(s_ots, pp + 1)
                if pp >= 1:
                    pe.wait_ge(s_od, pp)
                for it in range(2):
                    for q in range(2):
                        last = nc.tensor.transpose(banks(6)[:, (2 * it + q) * P:(2 * it + q + 1) * P],
                                                   OTS[:, pp % 2, q * S + it * P:q * S + (it + 1) * P], ident)
                last.then_inc(s_ott, 1)

            for n in range(4 * B + 4):
                if n < 4 * B:
                    scores0T(n)
                if 1 <= n <= 4 * B:
                    outputs0(n - 1)
                if n >= 3 and n % 2 == 1 and (n - 3) // 2 < 2 * B:
                    transpose_heads((n - 3) // 2)
                if n >= 6 and n % 4 == 2:
                    b = n // 4 - 1
                    take_misc("oT", b)
                    pe.wait_ge(s_od, 2 * b + 2)
                    for it in range(2):
                        last = nc.tensor.transpose(misc[:, it * P:(it + 1) * P], OD[:, b % 2, it, :], ident)
                    last.then_inc(s_mp7, 1)
                    pe.wait_ge(s_odt, b + 1)
                    if b == 0:
                        pe.wait_ge(d_late, 64)
                    for it in range(2):
                        last = mm(misc[:, S + it * P:S + (it + 1) * P], ODT[:, b % 2, it * P:(it + 1) * P],
                                  WO0[:, :], start=True, stop=True)
                    last.then_inc(s_mp7, 1)
                if n >= 7 and n % 4 == 3:
                    transpose_x(1, n // 4 - 1)

            def logits(n):
                if n == 0:
                    pe.wait_ge(s_p0, 4 * B)
                if n >= 2:
                    pe.wait_ge(s_te, n - 1)
                pe.wait_ge(s_xt, B + n // 2 + 1)
                xt = XT[:, n * P:(n + 1) * P]
                mm(banks(2 * (n % 2))[:, 0:306], xt, TG[:, 0:306], start=True, stop=True)
                mm(banks(2 * (n % 2) + 1)[:, 0:300], xt, TG[:, 306:606], start=True, stop=True).then_inc(s_lg, 1)

            def values(n):
                pe.wait_ge(s_pe, n + 1)
                if n >= 1:
                    pe.wait_ge(s_ptec, n)
                for t in range(ELT):
                    last = nc.tensor.transpose(banks(4, 640)[0:EL, t * P:(t + 1) * P],
                                               TE[:, n % 2, t * EL:(t + 1) * EL], ident)
                last.then_inc(s_pte, 1)
                if n == 0:
                    pe.wait_ge(s_od, 2 * B)
                if n >= 1:
                    pe.wait_ge(s_dl, n)
                mm(banks(6)[:, P:2 * P], XT[:, n * P:(n + 1) * P], WTD[:, 1, :], start=True, stop=True)
                pe.wait_ge(s_ptec, n + 1)
                for t in range(ELT):
                    last = mm(banks(6)[:, 0:P], PTE[:, n % 2, t, :], VP[:, t, :], start=(t == 0),
                              stop=(t == ELT - 1), skip_group_check=True)
                last.then_inc(s_acc, 1)

            for n in range(NT + 4):
                if n < NT:
                    logits(n)
                if 1 <= n <= NT:
                    values(n - 1)
                if n >= 4 and n % 2 == 0 and n // 2 - 2 < B:
                    transpose_x(2, n // 2 - 2)

            def event(ev):
                kind, b = ev[0], ev[1]
                if kind == "xT":
                    transpose_x(ev[1], ev[2])
                    return
                take_misc(*ev)
                if kind == "q":
                    j = ev[2]
                    pe.wait_ge(s_xt, 2 * B + b + 1)
                    for c in range(2):
                        last = mm(misc[:, c * S:(c + 1) * S], W1[:, 0, (2 * j + c) * P:(2 * j + c + 1) * P],
                                  XT[:, b * S:(b + 1) * S], start=True, stop=True)
                elif kind == "wo1":
                    pe.wait_ge(s_ot1, 2 * b + 2)
                    for it in range(2):
                        for c in range(4):
                            last = mm(misc[:, it * P:(it + 1) * P], OT1[:, b % 2, c, it * P:(it + 1) * P],
                                      WO1[:, c, :], start=(c == 0), stop=(c == 3))
                elif kind == "r1":
                    pe.wait_ge(s_xt, 3 * B + b + 1)
                    last = mm(misc[:, 0:NE], MS[:, b:b + 1].to_broadcast([P, P]), WR[:, :], start=True, stop=True)
                elif kind == "r2":
                    pe.wait_ge(s_oh, b + 1)
                    for k in range(3):
                        last = nc.tensor.transpose(misc[0:NE, k * P:(k + 1) * P], OH[:, b, k, :], ident)
                elif kind == "r3":
                    pe.wait_ge(s_oht, b + 1)
                    for f in range(FT):
                        last = mm(misc[:, 2 * f:2 * f + 2], B12[:, f * P:(f + 1) * P], OHT[:, b, 0:2, 0],
                                  start=True, stop=True)
                last.then_inc(s_mp7, 1)

            def scores1(n):
                b, c = divmod(n, 4)
                pe.wait_ge(s_q1, 2 * b + c // 2 + 1)
                if n >= 2:
                    pe.wait_ge(s_e1, n - 1)
                for it in range(2):
                    for h in range(2):
                        rows = slice(64 * h, 64 * h + 64)
                        last = mm(banks(2 * (n % 2) + h)[:, it * S:(it + 1) * S],
                                  QT1[rows, b % 2, c, it * P:(it + 1) * P], KT1[rows, c, b * S:(b + 1) * S],
                                  start=True, stop=True)
                last.then_inc(s_s1, 1)

            def transpose_p(n):
                pe.wait_ge(s_p1, n + 1)
                if n >= 1:
                    pe.wait_ge(s_pt1a, n)
                    pe.wait_ge(s_pt1d, n)
                for h in range(2):
                    for jt in range(2):
                        for it in range(2):
                            last = nc.tensor.transpose(
                                banks(4 + h)[:, jt * S + it * P:jt * S + (it + 1) * P],
                                PR[:, n % 3, h, it, jt * P:(jt + 1) * P], ident)
                last.then_inc(s_t1, 1)

            def outputs1(n):
                b, c = divmod(n, 4)
                pe.wait_ge(s_pt1a, n + 1)
                pe.wait_ge(s_pt1d, n + 1)
                if n >= 2 and n % 2 == 0:
                    pe.wait_ge(s_ot1, n // 2)
                for jt in range(2):
                    for h in range(2):
                        rows = slice(64 * h, 64 * h + 64)
                        last = mm(banks(6)[rows, (n % 2) * S:(n % 2 + 1) * S],
                                  V1[:, 2 * b + jt, (2 * c + h) * D1:(2 * c + h + 1) * D1],
                                  PT1[:, n % 3, h, jt, :], start=(jt == 0), stop=(jt == 1), skip_group_check=True)
                last.then_inc(s_av1, 1)

            for j in range(2):
                event(("q", 0, j))
            pe.wait_ge(s_te, NT)
            pe.wait_ge(s_dl, NT)
            for n in range(4 * B + 2):
                b, s = divmod(n, 4)
                if n < 4 * B:
                    scores1(n)
                if 1 <= n <= 4 * B:
                    transpose_p(n - 1)
                if n >= 2:
                    outputs1(n - 2)
                if n < 4 * B:
                    for ev in l1_events(b, s):
                        event(ev)
            for s in range(7):
                for ev in l1_events(B, s):
                    event(ev)

            def hidden(m):
                b, k = divmod(m, 2)
                if k == 0:
                    pe.wait_ge(d_w12[b], 32)
                if m == 0:
                    pe.wait_ge(s_e1, 4 * B)
                if m >= 2:
                    pe.wait_ge(s_g, m - 1)
                for f in range(FT):
                    last = mm(banks(2 * (m % 2), 1024)[:, f * S:(f + 1) * S], W12[:, m, f * P:(f + 1) * P],
                              XT[:, b * S:(b + 1) * S], start=True, stop=True)
                last.then_inc(s_h, 1)

            def expert_out(m):
                b, k = divmod(m, 2)
                if k == 0:
                    if b >= 2:
                        pe.wait_ge(s_yc, b - 1)
                    take_misc("base", b)
                    for t in range(2):
                        last = mm(misc[:, t * P:(t + 1) * P], OHT[:, b, 2, :], B12[:, F:F + P], start=True, stop=True)
                    last.then_inc(s_mp7, 1)
                pe.wait_ge(s_g, m + 1)
                for t in range(2):
                    for f in range(FT):
                        last = mm(banks(4 + b % 2)[:, k * S + t * P:k * S + (t + 1) * P],
                                  HT[:, m % 2, f, t * P:(t + 1) * P], W12[:, m, F + f * P:F + (f + 1) * P],
                                  start=(f == 0), stop=(f == FT - 1))
                last.then_inc(s_y, 1)

            for m in range(2 * B + 1):
                if m < 2 * B:
                    hidden(m)
                if m >= 1:
                    expert_out(m - 1)


def kernel(**inputs):
    import numpy as np
    import concourse.bacc as bacc
    from concourse.bass_utils import run_bass_kernel_spmd

    i = {k: np.asarray(v) for k, v in inputs.items()}
    cat = np.concatenate
    fp = np.float32
    c = np.zeros((P, NCONST), fp)
    c[:, C_ID:C_ID + P] = np.eye(P, dtype=fp)
    row, col = np.mgrid[0:P, 0:P]
    for it in range(2):
        keep = (col < row) | ((row == 0) & (col == 0) & (it == 0))
        c[:, C_MASK + it * P:C_MASK + (it + 1) * P] = np.where(keep, fp(0), fp(-BIG))
    flat = np.arange(EL)[:, None] + EL * np.arange(ELT)[None, :]
    c[:EL, C_L0:C_L0 + ELT] = (flat % NL != 0).astype(fp)
    c[:, C_W6:C_W6 + 6] = np.arange(NX, 0, -1, dtype=fp)
    c[:, C_IOTA:C_IOTA + NE] = np.arange(NE, dtype=fp)
    by_feature = lambda w: w.reshape(D, H0, D0).transpose(0, 2, 1).reshape(D, D)
    arrays = {
        "x": i["x"].reshape(B * S, D),
        "ctxT": i["ctx_1024"].reshape(B * S, D).T,
        "w0": np.stack([by_feature(i["L0_xattn_W_q"]), by_feature(i["L0_xattn_W_k"]), i["L0_xattn_W_v"]], 1),
        "wo0": i["L0_xattn_W_o"],
        "ab": cat([i["L0_ffn_A"].transpose(2, 0, 1).reshape(NR, NX * NL),
                   i["L0_ffn_B"].transpose(1, 0, 2).reshape(NR, NX * D)], 1),
        "wtd": np.stack([i["L0_ffn_wt_w"].T, i["L0_ffn_wd_w"].T], 1),
        "wgate": i["L0_ffn_w_gate"],
        "vecs": cat([np.stack([i["g_xattn"], i["g_ffn"]], 0).reshape(4)[[0, 1, 2, 3]], i["L0_xattn_b_o"],
                     i["L1_xattn_bo"], i["L0_ffn_wd_b"], i["L1_ffn_gamma"], i["L1_ffn_beta"],
                     i["L1_ffn_br"], i["L0_ffn_scale"]]),
        "cols": np.stack([i["L0_xattn_b_v"], i["L0_ffn_wt_b"]], 1),
        "w1": np.stack([i["L1_xattn_Wq"], i["L1_xattn_Wk"], i["L1_xattn_Wv"]], 1),
        "wo1": i["L1_xattn_Wo"].reshape(4, P, D).transpose(1, 0, 2),
        "wr": i["L1_ffn_Wr"],
        "b12": cat([i["L1_ffn_b1"], i["L1_ffn_b2"]], 1),
        "w12": cat([i["L1_ffn_W1"],
                    i["L1_ffn_W2"].reshape(NE, FT, P, D).transpose(0, 2, 1, 3).reshape(NE, P, F)], 2),
        "consts": c,
    }
    nc = bacc.Bacc("TRN2", target_bir_lowering=False, num_devices=1)
    feed, args = {}, []
    for name, a in arrays.items():
        a = np.ascontiguousarray(a)
        feed["in_" + name] = a
        args.append(nc.dram_tensor("in_" + name, a.shape, mybir.dt.from_np(a.dtype), kind="ExternalInput").ap())
    args.append(nc.dram_tensor("out_x", (B * S, D), mybir.dt.float32, kind="ExternalOutput").ap())
    args.append(nc.dram_tensor("qk_scr", (B, 2, 6, P, S), mybir.dt.bfloat16, kind="Internal").ap())
    args.append(nc.dram_tensor("m_scr", (B, 32, S), mybir.dt.bfloat16, kind="Internal").ap())
    build_program(nc, *args)
    r = run_bass_kernel_spmd(nc, [feed], core_ids=[0])
    return r.results[0]["out_x"].reshape(B, S, D)
```

```python
from contextlib import ExitStack

import concourse.bass as bass
from concourse import mybir

B, S, D = 4, 256, 128
P = 128
NT = B * S // P
H0, D0 = 16, 8
NX, NL, NR = 6, 100, 16
EL, ELT = 120, 5
D1 = 64
NE, F = 8, 512
FT = F // P
KR = 6 * D0
KV_LATE = 4 * B - 9
KV_BANK = [6] * 3 + [4, 5, 6] * 2 + [m % 2 for m in range(KV_LATE)]
KZ = 96
BIG = 1.0e30
EPS_LN = 1e-5
EPS_LOG = 1.1920928955078125e-07
V_G, V_BO0, V_BO1, V_WDB, V_GAM, V_BET, V_BR, V_SC = 0, 4, 132, 260, 388, 516, 644, 652
NVEC = 653
C_ID, C_MASK, C_L0, C_W6, C_IOTA = 0, 128, 384, 389, 395
NCONST = 403


M0 = -6
E0 = 17
A1 = E0 + 10
M1 = A1 + 17
STEPS = range(M0, M1 + 2 * B + 2)
ON_PE = ("mT", "oT", "wo0", "xT", "gate", "q", "wo1", "r1", "r2", "r3", "base")


def events(g, late):
    at = []

    def put(step, *ev):
        if step == g + 0.5 * late:
            at.append(ev)

    for b in range(B):
        put(M0 + 4 * b + 3.5, "mparts", b)
        put(M0 + 4 * b + 4.5, "mT", b)
    for b in range(B):
        put(M1 + 1 + 2 * b, "base", b)
    for b in range(B):
        put(4 * b + 7, "oT", b)
        put(4 * b + 7.5, "wo0", b)
        put(4 * b + 8.5, "ln", 1, b)
        put(4 * b + 10, "xT", 1, b)
        put(4 * b + 10.5, "gate", b)
    for b in range(B):
        put(E0 + 2 * b + 5, "exp0", b)
        put(E0 + 2 * b + 6.5, "log0", b)
        put(E0 + 2 * b + 7.5, "add0", b)
        put(E0 + 2 * b + 8.5, "ln", 2, b)
        put(E0 + 2 * b + 9, "xT", 2, b)
    for b in range(B):
        put(A1 + 4 * b - (2 if b else 0.5), "q", b, 0)
        put(A1 + 4 * b, "q", b, 1)
    for b in range(B):
        steps = {B - 2: (1, 1.5, 2.5, 2.5, 3, 3, 3.5, 5),
                 B - 1: (0.5, 1.5, 1.5, 2.5, 2.5, 2.5, 3.5, 4.5)}.get(b, (0, 1, 1.5, 2, 3, 4, 4.5, 5.5))
        for step, ev in zip(steps, (("wo1", b), ("ln", 3, b), ("xT", 3, b), ("r1", b), ("r1b", b),
                                    ("r1c", b), ("r2", b), ("r3", b))):
            put(A1 + 4 * b + {B - 2: 6, B - 1: 6}.get(b, 7) + step, *ev)
    for b in range(B):
        put(M1 + 1.5 + 2 * b, "fin0", b)
        put(M1 + 2.5 + 2 * b, "fin", b)
        put(M1 + 3.5 + 2 * b, "out", b)
    return at


def kvs(g):
    t = g - M0
    if t < 3:
        return [t]
    if t < 6:
        return [2 * t - 3, 2 * t - 2]
    if 4 * B <= t < 4 * B + KV_LATE:
        return [t - KV_LATE]
    return []


def misc_uses():
    uses = [("xT", 0, b) for b in range(B)]
    for g in STEPS:
        uses += [ev for late in (0, 1) for ev in events(g, late) if ev[0] in ON_PE]
    return uses


def build_program(nc, x, ctxT, w0, wo0, ab, wtd, wgate, vecs, cols, w1, wo1, wr, b12, w12, consts,
                  out, qk_scr):
    fp32, bf16, u32 = mybir.dt.float32, mybir.dt.bfloat16, mybir.dt.uint32
    ALU = mybir.AluOpType
    ACT = mybir.ActivationFunctionType
    AXX = mybir.AxisListType.X
    MISC = {u: i for i, u in enumerate(misc_uses())}
    READ = {u: i + 1 for i, u in enumerate(
        [u for u in misc_uses() if u[0] in ("wo0", "gate", "wo1", "r1", "base")])}

    ctx = ExitStack()
    with ctx:
        def sb(name, shape, dt=fp32):
            return ctx.enter_context(nc.sbuf_tensor(name, shape, dt))

        def sem(name):
            return ctx.enter_context(nc.semaphore(name))

        W0 = sb("W0", [P, 3, P])
        WO0 = sb("WO0", [P, P])
        AB = sb("AB", [NR, NX * (NL + P)])
        WTD = sb("WTD", [P, 2, P])
        TG = sb("TG", [P, 606])
        VEC = sb("VEC", [P, NVEC])
        COL = sb("COL", [P, 2])
        W1 = sb("W1", [P, 3, F])
        WO1 = sb("WO1", [P, 4, P])
        WR = sb("WR", [P, NE])
        B12 = sb("B12", [NE, F + P])
        CST = sb("CST", [P, NCONST])
        ident = CST[:, C_ID:C_ID + P]
        IDB = sb("IDB", [P, P], bf16)
        MSKB = sb("MSKB", [P, 2, P], bf16)
        HALF = sb("HALF", [P, 2])
        TG4 = sb("TG4", [P, 4])
        GT = sb("GT", [P, P])
        X = sb("X", [P, NT, D])
        XH = sb("XH", [P, NT, D])
        XT = sb("XT", [P, B * S])
        CT = sb("CT", [P, B * S])
        ST = sb("ST", [P, NT, 6])
        MV = sb("MV", [P, NT, 2])
        VE = sb("VE", [P, NT])
        RS = sb("RS", [P, NT])
        QK = sb("QK", [P, 2, B, H0 * S], bf16)
        ONE = sb("ONE", [2, S], bf16)
        QKZ = QK[0:KZ, :, :, :].rearrange("p a b n -> p a (b n)").bitcast(fp32)
        QKh = QK[:, :, :, :].rearrange("p a b (h t) -> p a b h t", h=H0)
        BIGF = QK[:, :, :, :].rearrange("p a b n -> p (a b n)").bitcast(fp32)
        PARTS = sb("PARTS", [P, 2, 12, S], bf16)
        VA = sb("VA", [P, NT, H0, 32])
        PT0 = sb("PT0", [P, 3, 4, 384])
        VAF = VA[:, :, :, :].rearrange("p a b c -> p (a b c)")
        PT0F = PT0[:, :, :, :].rearrange("p a b c -> p (a b c)")
        PARTF = PARTS[:, :, :, :].rearrange("p a b c -> p (a b c)").bitcast(fp32)
        RES = PT0F[:, 2048:3072].rearrange("p (a n) -> p a n", a=2)
        MX0 = sb("MX0", [P, B, 2, H0])
        MP = sb("MP", [P, B, 2, 2, H0], bf16)
        MT = sb("MT", [32, 2, S], bf16)
        OTS = PARTF[:, 0:1024].rearrange("p (a n) -> p a n", a=2)
        RC0 = sb("RC0", [P, 2, 8])
        OD = sb("OD", [P, 2, 2, P])
        ODT = sb("ODT", [P, 2, S])
        VT = sb("VT", [P, NX * NL])
        VP = sb("VP", [EL, ELT, P])
        MX6 = sb("MX6", [P, 2, 6])
        GM = sb("GM", [P, 2])
        T1 = sb("T1", [P, 2, 6])
        NB6 = sb("NB6", [P, B, 2, 6])
        SH6 = sb("SH6", [P, 2, 6])
        TE = BIGF[:, 8192:9992].rearrange("p (a n) -> p a n", a=3)
        SM0 = sb("SM0", [P, NT])
        RM0 = sb("RM0", [P, NT])
        PTE = VAF[0:EL, 2048:3328].rearrange("p (a t n) -> p a t n", a=2, t=ELT)
        DL = BIGF[:, 10240:10752].rearrange("p (a n) -> p a n", a=2)
        WS = BIGF[:, 10752:11008]
        CE = VAF[:, 3328:3584]
        ZE = VAF[:, 3584:3840]
        LNV = VAF[:, 3840:4096]
        KT1 = sb("KT1", [P, 4, B * S])
        V1 = sb("V1", [P, NT, F])
        V1F = V1[:, :, :].rearrange("p t n -> p (t n)").bitcast(bf16)
        SPLIT = [PARTS[:, 0], PARTS[:, 1]] + [V1F[:, 12 * S * i:12 * S * (i + 1)].rearrange(
            "p (k t) -> p k t", k=12) for i in range(2)]
        QT1 = VAF[:, 0:2048].rearrange("p (c h s) -> p c h s", c=4, h=2)
        OT1 = PT0F[:, 0:2048].rearrange("p (a c s) -> p a c s", a=2, c=4)
        PR = BIGF[:, 0:3072].rearrange("p (a h i j) -> p a h i j", a=3, h=2, i=2)
        PT1 = BIGF[:, 3072:6144].rearrange("p (a h j i) -> p a h j i", a=3, h=2, j=2)
        W12 = BIGF[:, 6144:14336].rearrange("p (m n) -> p m n", m=8)
        HT = BIGF[:, 14336:16384].rearrange("p (a f s) -> p a f s", a=2, f=FT)
        MX1 = sb("MX1", [P, 2, 4])
        NM1 = sb("NM1", [P, 2, 4])
        SM1 = sb("SM1", [P, 2, 4])
        RC1 = sb("RC1", [P, 2, 4])
        MS = sb("MS", [P, B])
        LG = sb("LG", [P, B, NE])
        MR = sb("MR", [P, B])
        ER = sb("ER", [P, B, NE])
        SR = sb("SR", [P, B])
        RR = sb("RR", [P, B])
        RW = sb("RW", [P, B, NE])
        TOP = sb("TOP", [P, B, 8])
        IDX = sb("IDX", [P, B, 8], u32)
        IDF = sb("IDF", [P, B, 8])
        DD = sb("DD", [P, B])
        E2 = sb("E2", [P, B])
        DEN = sb("DEN", [P, B])
        WK = sb("WK", [P, B, 2])
        OH = sb("OH", [P, B, 3, NE])
        OHT = sb("OHT", [NE, B, 3, P])
        B1S = sb("B1S", [P, B, FT, 2])
        Y = PARTF[:, 1024:1536].rearrange("p (a n) -> p a n", a=2)

        PS = ctx.enter_context(nc.psum_tensor("PS", [P, 8, 512], fp32))
        PSF = PS[:, :, :].rearrange("p k n -> p (k n)")

        def banks(k, n=512):
            return PSF[:, 512 * k:512 * k + n]

        misc = banks(7)

        d_x = [sem(f"d_x_{i}") for i in range(2)]
        d_ctx = [sem(f"d_ctx_{i}") for i in range(2)]
        d_c, d_w0, d_wt, d_vec, s_yg = map(sem, ("d_c", "d_w0", "d_wt", "d_vec", "s_yg"))
        d_w1, d_ab, d_late = map(sem, ("d_w1", "d_ab", "d_late"))
        s_cst, s_tanh, s_qz = map(sem, ("s_cst", "s_tanh", "s_qz"))
        s_xbo = sem("s_xbo")
        s_mv, s_rstd, s_xh, s_xt = map(sem, ("s_mv", "s_rstd", "s_xh", "s_xt"))
        s_mp7, s_mc7 = sem("s_misc_full"), sem("s_misc_free")
        s_qk, s_hi, s_res, s_mid, s_parts = map(sem, ("s_qk", "s_hi", "s_res", "s_mid", "s_parts"))
        s_v0p, s_v0, s_va0 = sem("s_v0p"), sem("s_v0"), sem("s_va0")
        d_one0, d_one, s_zero, s_zero_k, s_one = map(sem, ("d_one0", "d_one", "s_zero", "s_zero_k", "s_one"))
        d_scr = [sem(f"d_scr_{b}") for b in range(B)]
        d_qk = [sem(f"d_qk_{b}") for b in range(B)]
        d_shift = [sem(f"d_shift_{b}") for b in range(B)]
        s_s0, s_mx0, s_mparts, s_mt = map(sem, ("s_s0", "s_mx0", "s_mparts", "s_mt"))
        s_tok, s_tokc, s_vt, s_vtc, s_vp, s_vpc = map(sem, ("s_tok", "s_tokc", "s_vt", "s_vtc", "s_vp", "s_vpc"))
        s_rc1, s_p1p = sem("s_rc1"), sem("s_p1p")
        s_k1, s_k1c = sem("s_k1"), sem("s_k1c")
        s_sta, s_stb, s_pa, s_p0, s_pm, s_av0, s_ots, s_ott, s_od, s_odt = map(
            sem, ("s_sta", "s_stb", "s_pa", "s_p0", "s_pm", "s_av0", "s_ots", "s_ott", "s_od", "s_odt"))
        s_lg, s_te, s_pe, s_pte, s_ptec, s_acc, s_dl = map(
            sem, ("s_lg", "s_te", "s_pe", "s_pte", "s_ptec", "s_acc", "s_dl"))
        s_ce, s_cg, s_ln, s_ws = map(sem, ("s_ce", "s_cg", "s_ln", "s_ws"))
        s_s1, s_nm1, s_e1, s_p1, s_t1, s_pt1a, s_pt1d, s_av1, s_ot1 = map(
            sem, ("s_s1", "s_nm1", "s_e1", "s_p1", "s_t1", "s_pt1a", "s_pt1d", "s_av1", "s_ot1"))
        s_q1, s_lgr, s_er, s_idx, s_dd, s_e2, s_oh, s_oht, s_b1s = map(
            sem, ("s_q1", "s_lgr", "s_er", "s_idx", "s_dd", "s_e2", "s_oh", "s_oht", "s_b1s"))
        d_w12 = [sem(f"d_w12_{b}") for b in range(B)]
        s_h, s_g, s_y, s_yc, s_fin, d_out = map(sem, ("s_h", "s_g", "s_y", "s_yc", "s_fin", "d_out"))
        c_dve, c_pool = sem("c_dve"), sem("c_pool")

        def chain(eng, s):
            count = [0]

            def link(ins):
                count[0] += 1
                ins.then_inc(s, 1)
                eng.wait_ge(s, count[0])
            return link

        block = ctx.enter_context(nc.Block())

        @block.sync
        def _(sp):
            xr = x.rearrange("(t p) d -> p t d", p=P)
            sp.dma_start(X[:, 0:4, :], xr[:, 0:4, :]).then_inc(d_x[0], 16)
            half = B * S // 2
            sp.dma_start(W0[:, :, :], w0).then_inc(d_w0, 16)
            sp.dma_start(CT[:, 0:half], ctxT[:, 0:half]).then_inc(d_ctx[0], 16)
            sp.dma_start(X[:, 4:8, :], xr[:, 4:8, :]).then_inc(d_x[1], 16)
            sp.dma_start(CT[:, half:2 * half], ctxT[:, half:2 * half]).then_inc(d_ctx[1], 16)
            sp.dma_start(COL[:, :], cols).then_inc(d_wt, 16)
            sp.dma_start(AB[:, :], ab).then_inc(d_ab, 16)
            sp.dma_start(WTD[:, :, :], wtd).then_inc(d_ab, 16)
            sp.dma_start(TG[:, 300:306], wgate).then_inc(d_ab, 16)
            sp.dma_start(W1[:, :, :], w1).then_inc(d_w1, 16)

            def split_out(b):
                sp.wait_ge(s_parts, b + 1)
                sp.dma_start(qk_scr[b].rearrange("a k p t -> p (a k) t"),
                             SPLIT[b]).then_inc(d_scr[b], 16)

            def split_in(b):
                sp.wait_ge(s_zero, b + 1)
                sp.wait_ge(d_scr[b], 16)
                sp.dma_start(QK[0:KR, :, b, :],
                             qk_scr[b].rearrange("a k (r h) t -> (k r) a (h t)", h=H0)).then_inc(d_qk[b], 16)

            def ones(k, s):
                sp.dma_start(QK[KR:KR + 2, 1, k, :].rearrange("p b (h t) -> p (b h) t", t=S),
                             ONE[:, :].unsqueeze(1).to_broadcast([2, (k.stop - k.start) * H0, S])).then_inc(s, 16)

            sp.wait_ge(s_one, 1)
            sp.wait_ge(s_zero, 1)
            sp.wait_ge(s_zero_k, 1)
            ones(slice(0, 1), d_one0)
            for ready, parts in ((s_hi, ((0, 0), (0, 3), (0, 5), (6, 6), (6, 7), (6, 8))),
                                 (s_mid, ((1, 1), (1, 4), (9, 9), (9, 10))), (s_parts, ((2, 2), (11, 11)))):
                sp.wait_ge(ready, 1)
                for src, k in parts:
                    sp.dma_start(QK[k % 6 * D0:(k % 6 + 1) * D0, k // 6, 0, :].rearrange("r (h t) -> r h t", h=H0),
                                 SPLIT[0][:, src, :]).then_inc(d_qk[0], 16)
            split_out(1)
            split_out(2)
            sp.wait_ge(s_zero, B)
            ones(slice(1, B), d_one)
            split_in(1)
            split_out(3)
            split_in(2)
            split_in(3)
            sp.dma_start(WO0[:, :], wo0).then_inc(d_late, 16)
            sp.dma_start(WO1[:, :, :], wo1).then_inc(d_late, 16)
            sp.dma_start(WR[:, :], wr).then_inc(d_late, 16)
            sp.dma_start(B12[:, :], b12).then_inc(d_late, 16)
            for b in range(B):
                sp.wait_ge(s_mt, b + 1)
                sp.dma_start(QK[KR:KR + 2, 0, b, :].rearrange("k (h t) -> k h t", h=H0),
                             MT[:, b % 2, :]).then_inc(d_shift[b], 16)
            for b in range(B):
                sp.wait_ge(s_idx, b + 1)
                for k in range(2):
                    e = sp.value_load(IDX[0:1, b, k:k + 1], min_val=0, max_val=NE - 1)
                    sp.dma_start(W12[:, 2 * b + k, :],
                                 w12[bass.ds(e, 1)].rearrange("o p n -> (o p) n")).then_inc(d_w12[b], 16)
            for b in range(B):
                sp.wait_ge(s_fin, b + 1)
                sp.dma_start(out[b * S:(b + 1) * S].rearrange("(t p) d -> p t d", p=P),
                             X[:, 2 * b:2 * b + 2, :]).then_inc(d_out, 16)
            sp.wait_ge(d_out, 16 * B)

        @block.gpsimd
        def _(pool):
            link = chain(pool, c_pool)
            g_ = nc.gpsimd
            g_.memset(HALF[:, :], -0.5)
            g_.memset(ONE[:, :], 1.0).then_inc(s_one, 1)

            def zero_qk(b):
                w = H0 * S // 2
                g_.memset(QKZ[:, :, b * w:(b + 1) * w], 0.0).then_inc(s_zero, 1)

            def rstd(n):
                b = n % B
                pool.wait_ge(s_mv, n + 1)
                link(g_.tensor_scalar_add(VE[:, 2 * b:2 * b + 2], MV[:, 2 * b:2 * b + 2, 1], EPS_LN))
                g_.tensor_tensor(RS[:, 2 * b:2 * b + 2], VE[:, 2 * b:2 * b + 2], HALF[:, :],
                                 ALU.pow).then_inc(s_rstd, 1)

            def add_bias(n, off):
                b = n % B
                xs = X[:, 2 * b:2 * b + 2, :]
                g_.tensor_tensor(xs, xs, VEC[:, off:off + D].unsqueeze(1).to_broadcast([P, 2, D]),
                                 ALU.add).then_inc(s_xbo, 1)

            g_.memset(QKZ[:, 0, 0:H0 * S // 2], 0.0).then_inc(s_zero, 1)
            for b in range(B):
                rstd(b)
            for b in range(1, B):
                zero_qk(b)
            g_.memset(VA[:, :, :, 8:9], 1.0)
            g_.memset(VA[:, :, :, 9:32], 0.0).then_inc(s_va0, 1)
            pool.wait_ge(d_vec, 16)
            pool.wait_ge(s_tanh, 1)
            for off, gate in ((V_BO0, 0), (V_BO1, 1), (V_BET, 3)):
                g_.tensor_tensor(VEC[:, off:off + D], VEC[:, off:off + D],
                                 TG4[:, gate:gate + 1].to_broadcast([P, D]), ALU.mult)
            link(g_.tensor_tensor(GT[:, :], VEC[:, V_GAM:V_GAM + D],
                                  TG4[:, 3:4].to_broadcast([P, D]), ALU.mult))
            pool.wait_ge(s_xh, B)
            for b in range(B):
                add_bias(b, V_BO0)

            def mask0(n):
                pool.wait_ge(s_p0, n + 1)
                pt = PT0[:, n % 3]
                g_.affine_select(out=pt[:, :, 0:128], in_=pt[:, :, 0:128], compare_op=ALU.is_gt, fill=0.0,
                                 base=1, pattern=[[0, 4], [126, 128]], channel_multiplier=-127)
                g_.affine_select(out=pt[:, :, 256:384], in_=pt[:, :, 256:384], compare_op=ALU.is_gt,
                                 fill=0.0, base=0, pattern=[[0, 4], [1, 128]],
                                 channel_multiplier=-1).then_inc(s_pm, 1)

            def normalise1(n):
                pool.wait_ge(s_rc1, n + 1)
                pr = PR[:, n % 3, 1]
                g_.tensor_tensor(pr, pr, RC1[:, n % 2, 2:4].unsqueeze(2).to_broadcast([P, 2, S]),
                                 ALU.mult).then_inc(s_p1p, 1)

            for g in STEPS:
                if 0 <= g < 4 * B:
                    mask0(g)
                if g == E0 + 5:
                    pool.wait_ge(s_av0, 4 * B)
                    g_.memset(VAF[:, 0:2048], 0.0).then_inc(s_qz, 1)
                if 1 <= g - A1 < 4 * B + 1:
                    normalise1(g - A1 - 1)
                for ev in events(g, 0) + events(g, 1):
                    kind, b = ev[0], ev[-1]
                    if kind == "wo0":
                        rstd(B + b)
                    if kind == "exp0":
                        pool.wait_ge(s_ce, b + 1)
                        link(g_.tensor_scalar(ZE[:, :], CE[:, :], 0.0, EPS_LOG, ALU.is_equal, ALU.mult))
                        g_.tensor_tensor(CE[:, :], CE[:, :], ZE[:, :], ALU.add).then_inc(s_cg, 1)
                    if kind == "log0":
                        pool.wait_ge(s_ln, b + 1)
                        g_.tensor_tensor(WS, XH[:, 2 * b:2 * b + 2, :].rearrange("p t d -> p (t d)"), LNV,
                                         ALU.add).then_inc(s_ws, 1)
                    if kind == "add0":
                        rstd(2 * B + b)
                    if kind == "wo1":
                        rstd(3 * B + b)
                    if kind == "ln" and ev[1] >= 2:
                        pool.wait_ge(s_xh, ev[1] * B + b + 1)
                        add_bias((ev[1] - 1) * B + b, {2: V_BO1, 3: V_BET}[ev[1]])
                    if kind == "fin":
                        rstd(4 * B + b)

        @block.scalar
        def _(act):
            a = nc.scalar
            act.dma_start(CST[:, :], consts).then_inc(d_c, 16)
            act.dma_start(VEC[:, :], vecs.partition_broadcast(P)).then_inc(d_vec, 16)

            def wait_misc(*use):
                act.wait_ge(s_mp7, MISC[use] + 1)

            def copy_xT(layer, b):
                wait_misc("xT", layer, b)
                kw = {"accum_out": MS[:, b:b + 1]} if layer == 3 else {}
                a.activation(XT[:, b * S:(b + 1) * S], misc[:, 0:S], ACT.Identity, **kw).then_inc(s_xt, 1)

            act.wait_ge(d_vec, 16)
            a.activation(TG4[:, :], VEC[:, V_G:V_G + 4], ACT.Tanh).then_inc(s_tanh, 1)
            a.preload_act_table_set("natural_log_exp_and_others")
            act.wait_ge(d_c, 16)
            a.activation(IDB[:, :], ident, ACT.Copy)
            a.activation(MSKB[:, :, :], CST[:, C_MASK:C_MASK + 2 * P].rearrange("p (a b) -> p a b", a=2),
                         ACT.Copy).then_inc(s_cst, 1)
            def project(b):
                copy_xT(0, b)
                act.wait_ge(s_qk, b + 1)
                a.activation(SPLIT[b][:, 0:7:6], banks(4 + b % 2).rearrange("p (a t) -> p a t", a=2),
                             ACT.Copy).then_inc(s_hi, 1)
                act.wait_ge(s_v0p, b + 1)
                a.activation(VA[:, 2 * b:2 * b + 2, :, 0:8],
                             banks(6, 256).rearrange("p (t h d) -> p t h d", t=2, h=H0),
                             ACT.Copy).then_inc(s_v0, 1)

            def expert_tokens(t):
                if t == 0:
                    act.wait_ge(s_tok, 1)
                    a.activation(TG[:, 0:300], banks(2, 300), ACT.Copy)
                    a.activation(TG[:, 306:606], banks(3, 300), ACT.Copy).then_inc(s_tokc, 1)
                if t == 1:
                    act.wait_ge(s_vt, 1)
                    act.wait_ge(d_wt, 16)
                    a.activation(VT[:, 0:300], banks(0, 300), ACT.Identity, bias=COL[:, 1:2])
                    a.activation(VT[:, 300:600], banks(1, 300), ACT.Identity, bias=COL[:, 1:2]).then_inc(s_vtc, 1)
                if t == 2:
                    act.wait_ge(s_vp, 1)
                    for i in range(ELT):
                        a.activation(VP[:, i, :], banks(2, 640)[0:EL, i * P:(i + 1) * P], ACT.Copy,
                                     scale=CST[0:EL, C_L0 + i:C_L0 + i + 1]).then_inc(s_vpc, 1)

            for b in range(B):
                project(b)
                if b == 1:
                    expert_tokens(0)
            expert_tokens(1)

            def kv(m):
                act.wait_ge(s_k1, m + 1)
                b, j = divmod(m, 4)
                src = banks(KV_BANK[m])
                if j < 2:
                    dst = KT1[:, 2 * j:2 * j + 2, b * S:(b + 1) * S]
                    src = src.rearrange("p (c t) -> p c t", c=2)
                else:
                    dst = V1[:, 2 * b + j - 2, :]
                    if m == 2:
                        for i in (2, 3):
                            act.wait_ge(d_scr[i], 16)
                a.activation(dst, src, ACT.Copy).then_inc(s_k1c, 1)

            def exps0(n):
                if n >= 3:
                    act.wait_ge(s_av0, n - 2)
                act.wait_ge(s_sta, n + 1)
                a.activation(PT0[:, n % 3, :, 0:256],
                             banks(2, 1024).rearrange("p (h i) -> p h i", h=4),
                             ACT.Exp, scale=D0 ** -0.5).then_inc(s_pa, 1)
                act.wait_ge(s_stb, n + 1)
                a.activation(PT0[:, n % 3, :, 256:384],
                             banks(4).rearrange("p (h i) -> p h i", h=4),
                             ACT.Exp, scale=D0 ** -0.5).then_inc(s_p0, 1)

            def probs_te(m):
                act.wait_ge(s_pte, m + 1)
                a.activation(PTE[:, m % 2].rearrange("p t n -> p (t n)"), banks(4, 640)[0:EL, :],
                             ACT.Copy).then_inc(s_ptec, 1)

            def exps_te(n):
                act.wait_ge(s_te, n + 1)
                a.activation(TE[:, n % 3, :], TE[:, n % 3, :], ACT.Exp, scale=D ** -0.5,
                             accum_out=SM0[:, n:n + 1]).then_inc(s_pe, 1)

            def exps1(n):
                act.wait_ge(s_nm1, n + 1)
                for h in range(2):
                    for it in range(2):
                        last = a.activation(PR[:, n % 3, h, it, :],
                                            banks(2 * (n % 2) + h)[:, it * S:(it + 1) * S], ACT.Exp,
                                            scale=D1 ** -0.5, bias=NM1[:, n % 2, 2 * h + it:2 * h + it + 1],
                                            accum_out=SM1[:, n % 2, 2 * h + it:2 * h + it + 1])
                last.then_inc(s_e1, 1)

            def probs1(n):
                act.wait_ge(s_t1, n + 1)
                a.activation(PT1[:, n % 3, 1].rearrange("p j i -> p (j i)"), banks(5),
                             ACT.Copy).then_inc(s_pt1a, 1)

            def outs1(p):
                act.wait_ge(s_av1, 2 * p + 2)
                a.activation(OT1[:, (p // 2) % 2, 2 * (p % 2):2 * (p % 2) + 2, :],
                             banks(6).rearrange("p (c t) -> p c t", c=2), ACT.Copy).then_inc(s_ot1, 1)

            def gelu(m):
                act.wait_ge(s_b1s, m // 2 + 1)
                act.wait_ge(s_h, m + 1)
                if m >= 2:
                    act.wait_ge(s_y, m - 1)
                for f in range(FT):
                    last = a.activation(HT[:, m % 2, f, :], banks(2 * (m % 2), 1024)[:, f * S:(f + 1) * S],
                                        ACT.Gelu, bias=B1S[:, m // 2, f, m % 2:m % 2 + 1])
                last.then_inc(s_g, 1)

            def event(ev):
                kind, b = ev[0], ev[-1]
                if kind == "mT":
                    wait_misc("mT", b)
                    if b >= 2:
                        act.wait_ge(d_shift[b - 2], 16)
                    a.activation(MT[:, b % 2, :], misc[0:32, 0:128].bitcast(bf16), ACT.Copy).then_inc(s_mt, 1)
                if kind == "oT":
                    wait_misc("oT", b)
                    a.activation(ODT[:, b % 2, :], misc[:, 0:S], ACT.Identity, bias=COL[:, 0:1]).then_inc(s_odt, 1)
                if kind == "xT":
                    copy_xT(ev[1], b)
                if kind == "exp0":
                    act.wait_ge(s_dl, 2 * b + 2)
                    if b >= 1:
                        act.wait_ge(s_ln, b)
                    a.activation(CE[:, :], DL[:, b % 2, :], ACT.Exp, scale=VEC[:, V_SC:V_SC + 1]).then_inc(s_ce, 1)
                if kind == "log0":
                    act.wait_ge(s_cg, b + 1)
                    if b >= 1:
                        act.wait_ge(s_ws, b)
                    a.activation(LNV[:, :], CE[:, :], ACT.Ln).then_inc(s_ln, 1)
                if kind == "q":
                    _, b, j = ev
                    if b == 0 and j == 0:
                        act.wait_ge(s_qz, 1)
                    wait_misc("q", b, j)
                    for h in range(2):
                        rows = slice(64 * h, 64 * h + 64)
                        last = a.activation(QT1[rows, 2 * j:2 * j + 2, h, :],
                                            misc[rows].rearrange("p (c t) -> p c t", c=2), ACT.Copy)
                    last.then_inc(s_q1, 1)
                if kind == "r1b":
                    act.wait_ge(s_lgr, b + 1)
                    a.activation(ER[:, b, :], LG[:, b, :], ACT.Exp, bias=MR[:, b:b + 1],
                                 accum_out=SR[:, b:b + 1]).then_inc(s_er, 1)
                if kind == "r1c":
                    act.wait_ge(s_dd, b + 1)
                    a.activation(E2[:, b:b + 1], DD[:, b:b + 1], ACT.Exp).then_inc(s_e2, 1)

            for g in STEPS:
                if 0 <= g < 4 * B:
                    exps0(g)
                for ev in events(g, 0):
                    event(ev)
                if g == M0:
                    expert_tokens(2)
                for m in kvs(g):
                    kv(m)
                if E0 < g < E0 + 1 + NT:
                    exps_te(g - E0 - 1)
                if E0 + 2 <= g < E0 + 2 + NT:
                    probs_te(g - E0 - 2)
                n = g - A1
                if 2 <= n < 4 * B + 2:
                    probs1(n - 2)
                if n >= 4 and n % 2 == 0 and n < 4 * B + 4:
                    outs1((n - 4) // 2)
                if 0 <= n < 4 * B:
                    exps1(n)
                if M1 <= g < M1 + 2 * B:
                    gelu(g - M1)
                for ev in events(g, 1):
                    event(ev)

        @block.vector
        def _(dve):
            v = nc.vector
            link = chain(dve, c_dve)

            def wait_misc(*use):
                dve.wait_ge(s_mp7, MISC[use] + 1)

            def stats(src):
                b, tiles = src
                for t in range(2):
                    last = v.bn_stats(ST[:, 2 * b + t, :], tiles[t])
                link(last)
                for t in (2 * b, 2 * b + 1):
                    last = v.bn_aggr(MV[:, t, :], ST[:, t, :])
                last.then_inc(s_mv, 1)

            def x_tiles(b):
                return b, (X[:, 2 * b, :], X[:, 2 * b + 1, :])

            def apply_norm(layer, b):
                dve.wait_ge(s_rstd, B * layer + b + 1)
                for t in (2 * b, 2 * b + 1):
                    last = v.tensor_scalar(XH[:, t, :], X[:, t, :], MV[:, t, 0:1], RS[:, t:t + 1],
                                           ALU.subtract, ALU.mult)
                last.then_inc(s_xh, 1)

            v.memset(QKZ[:, 1, 0:H0 * S // 2], 0.0).then_inc(s_zero_k, 1)
            for half in ((0, 1), (2, 3)):
                dve.wait_ge(d_x[half[0] // 2], 16)
                for b in half:
                    stats(x_tiles(b))
                for b in half:
                    apply_norm(0, b)
            for b in range(B):
                dve.wait_ge(s_hi, b + 1)
                ps = banks(4 + b % 2).rearrange("p (a t) -> p a t", a=2)
                res = RES[:, b % 2, :].rearrange("p (a t) -> p a t", a=2)
                pt = SPLIT[b]
                v.tensor_tensor(res, ps, pt[:, 0:7:6], ALU.subtract).then_inc(s_res, 1)
                if b > 0:
                    v.tensor_copy(pt[:, 3:6:2], pt[:, 0:1].to_broadcast([P, 2, S]))
                    v.tensor_copy(pt[:, 7:9], pt[:, 6:7].to_broadcast([P, 2, S]))
                dve.wait_ge(s_res, b + 1)
                v.tensor_copy(pt[:, 1:10:8], res).then_inc(s_mid, 1)
                dve.wait_ge(s_mid, b + 1)
                if b > 0:
                    v.tensor_copy(pt[:, 4:11:6], pt[:, 1:10:8])
                v.tensor_tensor(pt[:, 2:12:9], res, pt[:, 1:10:8], ALU.subtract).then_inc(s_parts, 1)

            def maxima0(n):
                b, u = divmod(n, 12)
                dve.wait_ge(s_s0, n + 1)
                if u < 8:
                    dst, w = MX0[:, b, 1, 2 * u:2 * u + 2], S
                else:
                    dst, w = MX0[:, b, 0, 4 * (u - 8):4 * (u - 8) + 4], P
                v.tensor_reduce(dst, banks(n % 2).rearrange("p (h j) -> p h j", j=w),
                                AXX, ALU.max, negate=True).then_inc(s_mx0, 1)

            def heads_out(pp):
                dve.wait_ge(s_av0, 2 * pp + 2)
                v.tensor_copy(OTS[:, pp % 2, :], banks(5)).then_inc(s_ots, 1)

            def heads_norm(pp):
                b, half = divmod(pp, 2)
                dve.wait_ge(s_ott, pp + 1)
                z = banks(6).rearrange("p (i h c) -> p i h c", i=2, h=8)
                link(v.reciprocal(RC0[:, :, :], z[:, :, :, 8]))
                v.tensor_tensor(OD[:, b % 2, :, 64 * half:64 * half + 64].rearrange("p i (h d) -> p i h d", h=8),
                                z[:, :, :, 0:8], RC0[:, :, :].unsqueeze(3).to_broadcast([P, 2, 8, 8]),
                                ALU.mult).then_inc(s_od, 1)

            def add_wo(use, b, gate, off, nbias):
                wait_misc(use, b)
                dve.wait_ge(s_xbo, nbias)
                xs = X[:, 2 * b:2 * b + 2, :].rearrange("p t d -> p (t d)")
                ins = v.scalar_tensor_tensor(xs, misc[:, off:off + S], TG4[:, gate:gate + 1], xs, ALU.mult, ALU.add)
                ins.then_inc(s_mc7, 1)
                dve.wait_ge(s_mc7, READ[(use, b)])
                stats(x_tiles(b))

            def prepare_te(n):
                k = n % 2
                dve.wait_ge(s_lg, n + 1)
                lg = banks(2 * k, 1024).rearrange("p (a c) -> p a c", a=2)[:, :, 0:300].rearrange(
                    "p a (e l) -> p a e l", e=3)
                link(v.tensor_reduce(MX6[:, k, :], lg, AXX, ALU.max))
                link(v.tensor_tensor(SH6[:, k, :], MX6[:, k, :], NB6[:, n // 2, k, :], ALU.add))
                if n >= 3:
                    dve.wait_ge(s_pte, n - 2)
                v.tensor_tensor(TE[:, n % 3, :].rearrange("p (a e l) -> p a e l", a=2, e=3), lg,
                                SH6[:, k, :].rearrange("p (a e) -> p a e", a=2).unsqueeze(3).to_broadcast(
                                    [P, 2, 3, NL]), ALU.subtract).then_inc(s_te, 1)

            def finish_te(n):
                dve.wait_ge(s_acc, n + 1)
                if n >= 4:
                    dve.wait_ge(s_ce, n // 2 - 1)
                dl = DL[:, (n // 2) % 2, (n % 2) * D:(n % 2 + 1) * D]
                acc = banks(6)
                v.reciprocal(RM0[:, n:n + 1], SM0[:, n:n + 1])
                link(v.tensor_tensor(dl, acc[:, D:2 * D], VEC[:, V_WDB:V_WDB + D], ALU.add))
                v.scalar_tensor_tensor(dl, acc[:, 0:D], RM0[:, n:n + 1], dl, ALU.mult, ALU.add).then_inc(s_dl, 1)

            def maxima1(n):
                k = n % 2
                dve.wait_ge(s_s1, n + 1)
                link(v.tensor_reduce(MX1[:, k, :], banks(2 * k, 1024).rearrange("p (c j) -> p c j", j=S),
                                     AXX, ALU.max, negate=True))
                v.tensor_scalar(NM1[:, k, :], MX1[:, k, :], D1 ** -0.5, None, ALU.mult).then_inc(s_nm1, 1)

            def normalise1(n):
                k = n % 2
                dve.wait_ge(s_e1, n + 1)
                v.reciprocal(RC1[:, k, :], SM1[:, k, :]).then_inc(s_rc1, 1)
                dve.wait_ge(s_rc1, n + 1)
                for it in range(2):
                    pr = PR[:, n % 3, 0, it, :]
                    last = v.tensor_scalar(pr, pr, RC1[:, k, it:it + 1], None, ALU.mult)
                last.then_inc(s_p1, 1)

            def probs1(n):
                dve.wait_ge(s_t1, n + 1)
                v.tensor_copy(PT1[:, n % 3, 0].rearrange("p j i -> p (j i)"), banks(4)).then_inc(s_pt1d, 1)

            def event(ev):
                kind, b = ev[0], ev[-1]
                xs = X[:, 2 * b:2 * b + 2, :]
                if kind == "mparts":
                    dve.wait_ge(s_mx0, 12 * b + 12)
                    link(v.tensor_copy(MP[:, b, :, 0, :], MX0[:, b]))
                    v.tensor_tensor(MP[:, b, :, 1, :], MX0[:, b], MP[:, b, :, 0, :],
                                    ALU.subtract).then_inc(s_mparts, 1)
                if kind == "wo0":
                    add_wo("wo0", b, 0, S, b + 1)
                if kind == "wo1":
                    add_wo("wo1", b, 1, 0, B + b + 1)
                if kind == "ln":
                    apply_norm(ev[1], b)
                if kind == "gate":
                    wait_misc("gate", b)
                    gate = misc[:, 0:12].rearrange("p (t e) -> p t e", t=2)
                    v.tensor_copy(T1[:, :, :], gate).then_inc(s_mc7, 1)
                    dve.wait_ge(s_mc7, READ[("gate", b)])
                    link(v.tensor_reduce(GM[:, :], T1[:, :, :], AXX, ALU.max))
                    link(v.tensor_tensor(T1[:, :, :], T1[:, :, :], GM[:, :].unsqueeze(2).to_broadcast([P, 2, 6]),
                                         ALU.is_ge))
                    link(v.tensor_tensor(T1[:, :, :], T1[:, :, :],
                                         CST[:, C_W6:C_W6 + 6].unsqueeze(1).to_broadcast([P, 2, 6]), ALU.mult))
                    link(v.tensor_reduce(GM[:, :], T1[:, :, :], AXX, ALU.max))
                    link(v.tensor_tensor(T1[:, :, :], T1[:, :, :], GM[:, :].unsqueeze(2).to_broadcast([P, 2, 6]),
                                         ALU.is_lt))
                    link(v.tensor_scalar(NB6[:, b, :, :], T1[:, :, :], BIG, None, ALU.mult))
                if kind == "add0":
                    dve.wait_ge(s_ws, b + 1)
                    xf = xs.rearrange("p t d -> p (t d)")
                    link(v.scalar_tensor_tensor(xf, WS[:, :], TG4[:, 2:3], xf, ALU.mult, ALU.add))
                    stats(x_tiles(b))
                if kind == "r1":
                    wait_misc("r1", b)
                    v.scalar_tensor_tensor(LG[:, b, :], misc[:, 0:NE], 1.0 / S, VEC[:, V_BR:V_BR + NE],
                                           ALU.mult, ALU.add).then_inc(s_mc7, 1)
                    dve.wait_ge(s_mc7, READ[("r1", b)])
                    v.tensor_reduce(MR[:, b:b + 1], LG[:, b, :], AXX, ALU.max, negate=True).then_inc(s_lgr, 1)
                if kind == "r1b":
                    dve.wait_ge(s_er, b + 1)
                    link(v.reciprocal(RR[:, b:b + 1], SR[:, b:b + 1]))
                    link(v.tensor_scalar(RW[:, b, :], ER[:, b, :], RR[:, b:b + 1], None, ALU.mult))
                    link(v.max(TOP[:, b, :], RW[:, b, :]))
                    v.tensor_tensor(DD[:, b:b + 1], TOP[:, b, 1:2], TOP[:, b, 0:1], ALU.subtract).then_inc(s_dd, 1)
                    v.max_index(IDX[:, b, :], TOP[:, b, :], RW[:, b, :]).then_inc(s_idx, 1)
                    dve.wait_ge(s_idx, b + 1)
                    link(v.tensor_copy(IDF[:, b, :], IDX[:, b, :]))
                    for k in range(2):
                        v.tensor_scalar(OH[:, b, k, :], CST[:, C_IOTA:C_IOTA + NE], IDF[:, b, k:k + 1], None,
                                        ALU.is_equal)
                if kind == "r1c":
                    dve.wait_ge(s_e2, b + 1)
                    link(v.tensor_scalar(DEN[:, b:b + 1], E2[:, b:b + 1], 1.0, None, ALU.add))
                    link(v.reciprocal(WK[:, b, 0:1], DEN[:, b:b + 1]))
                    link(v.tensor_tensor(WK[:, b, 1:2], E2[:, b:b + 1], WK[:, b, 0:1], ALU.mult))
                    link(v.tensor_scalar(OH[:, b, 2, :], OH[:, b, 0, :], WK[:, b, 0:1], None, ALU.mult))
                    v.scalar_tensor_tensor(OH[:, b, 2, :], OH[:, b, 1, :], WK[:, b, 1:2], OH[:, b, 2, :],
                                           ALU.mult, ALU.add).then_inc(s_oh, 1)
                if kind == "r2":
                    wait_misc("r2", b)
                    v.tensor_copy(OHT[:, b].rearrange("e k p -> e (k p)"), misc[0:NE, 0:3 * P]).then_inc(s_oht, 1)
                if kind == "r3":
                    wait_misc("r3", b)
                    v.tensor_copy(B1S[:, b].rearrange("p f k -> p (f k)"), misc[:, 0:2 * FT]).then_inc(s_b1s, 1)
                yb = Y[:, b % 2, :]
                if kind == "base":
                    wait_misc("base", b)
                    v.tensor_tensor(yb, misc[:, 0:S], XH[:, 2 * b:2 * b + 2, :].rearrange("p t d -> p (t d)"),
                                    ALU.add).then_inc(s_mc7, 1)
                if kind in ("fin0", "fin"):
                    k = int(kind == "fin")
                    if k == 0:
                        dve.wait_ge(s_mc7, READ[("base", b)])
                    dve.wait_ge(s_y, 2 * b + k + 1)
                    v.scalar_tensor_tensor(yb, banks(4 + k, S), WK[:, b, k:k + 1], yb, ALU.mult,
                                           ALU.add).then_inc(s_yc, 1)
                    dve.wait_ge(s_yc, 2 * b + k + 1)
                if kind == "fin":
                    stats((b, (yb[:, 0:D], yb[:, D:2 * D])))
                    dve.wait_ge(s_mv, 4 * B + b + 1)
                    for t in range(2):
                        yt = yb[:, t * D:(t + 1) * D]
                        v.scalar_tensor_tensor(yt, yt, MV[:, 2 * b + t, 0:1], GT[:, :], ALU.subtract,
                                               ALU.mult).then_inc(s_yg, 1)
                if kind == "out":
                    dve.wait_ge(s_rstd, 4 * B + b + 1)
                    dve.wait_ge(s_yg, 2 * b + 2)
                    dve.wait_ge(s_xbo, 2 * B + b + 1)
                    for t in range(2):
                        last = v.scalar_tensor_tensor(xs[:, t, :], yb[:, t * D:(t + 1) * D],
                                                      RS[:, 2 * b + t:2 * b + t + 1], xs[:, t, :], ALU.mult, ALU.add)
                    last.then_inc(s_fin, 1)

            for g in STEPS:
                n = g - A1
                if g < M0 + 4 * B:
                    for i in range(3):
                        maxima0(3 * (g - M0) + i)
                if g >= 3 and g % 2 == 1 and (g - 3) // 2 < 2 * B:
                    heads_out((g - 3) // 2)
                if g >= 4 and g % 2 == 0 and (g - 4) // 2 < 2 * B:
                    heads_norm((g - 4) // 2)
                if E0 + 4 <= g < E0 + 4 + NT:
                    finish_te(g - E0 - 4)
                for ev in events(g, 0):
                    if n < 0:
                        event(ev)
                if E0 <= g < E0 + NT:
                    prepare_te(g - E0)
                if 0 <= n < 4 * B:
                    maxima1(n)
                for ev in events(g, 0):
                    if n >= 0:
                        event(ev)
                if 1 <= n < 4 * B + 1:
                    normalise1(n - 1)
                if 2 <= n < 4 * B + 2:
                    probs1(n - 2)
                for ev in events(g, 1):
                    event(ev)

        @block.tensor
        def _(pe):
            mm = nc.tensor.matmul
            ORDER = misc_uses()

            def take_misc(*use):
                i = MISC[use]
                if i == 0:
                    return
                last = ORDER[i - 1]
                kind, b = last[0], last[-1]
                if kind == "xT":
                    pe.wait_ge(s_xt, B * last[1] + b + 1)
                elif kind == "mT":
                    pe.wait_ge(s_mt, b + 1)
                elif kind == "oT":
                    pe.wait_ge(s_odt, b + 1)
                elif kind == "q":
                    pe.wait_ge(s_q1, 2 * last[1] + last[2] + 1)
                elif kind == "r2":
                    pe.wait_ge(s_oht, b + 1)
                elif kind == "r3":
                    pe.wait_ge(s_b1s, b + 1)
                else:
                    pe.wait_ge(s_mc7, READ[last])

            def transpose_x(layer, b):
                take_misc("xT", layer, b)
                pe.wait_ge(s_xh, B * layer + b + 1)
                for t in range(2):
                    last = nc.tensor.transpose(misc[:, t * P:(t + 1) * P], XH[:, 2 * b + t, :], ident)
                last.then_inc(s_mp7, 1)

            def project(b):
                transpose_x(0, b)
                cols = slice(b * S, (b + 1) * S)
                if b == 0:
                    pe.wait_ge(d_w0, 16)
                if b % 2 == 0:
                    pe.wait_ge(d_ctx[b // 2], 16)
                if b >= 2:
                    pe.wait_ge(s_parts, b - 1)
                bank = banks(4 + b % 2)
                mm(bank[:, S:2 * S], W0[:, 1, :], CT[:, cols], start=True, stop=True)
                pe.wait_ge(s_xt, b + 1)
                mm(bank[:, 0:S], W0[:, 0, :], XT[:, cols], start=True, stop=True).then_inc(s_qk, 1)
                if b >= 1:
                    pe.wait_ge(s_v0, b)
                for t in range(2):
                    last = mm(banks(6)[:, t * P:(t + 1) * P], CT[:, b * S + t * P:b * S + (t + 1) * P],
                              W0[:, 2, :], start=True, stop=True)
                last.then_inc(s_v0p, 1)

            def expert_tokens(t):
                if t == 0:
                    pe.wait_ge(d_ab, 48)
                    for e in range(NX):
                        last = mm(banks(2 + e // 3)[:, (e % 3) * NL:(e % 3 + 1) * NL],
                                  AB[:, NX * NL + e * P:NX * NL + (e + 1) * P], AB[:, e * NL:(e + 1) * NL],
                                  start=True, stop=True)
                    last.then_inc(s_tok, 1)
                if t == 1:
                    pe.wait_ge(s_tokc, 1)
                    for i in range(2):
                        last = mm(banks(i)[:, 0:300], WTD[:, 0, :], TG[:, 306 * i:306 * i + 300],
                                  start=True, stop=True)
                    last.then_inc(s_vt, 1)
                if t == 2:
                    pe.wait_ge(s_vtc, 1)
                    for i in range(ELT):
                        last = mm(banks(2, 640)[0:EL, i * P:(i + 1) * P], VT[:, i * EL:(i + 1) * EL], WTD[:, 1, :],
                                  start=True, stop=True)
                    last.then_inc(s_vp, 1)

            pe.wait_ge(d_c, 16)
            for b in range(B):
                project(b)
                if b == 1:
                    expert_tokens(0)
            expert_tokens(1)

            def kv(m):
                b, j = divmod(m, 4)
                if m == 0:
                    pe.wait_ge(d_w1, 16)
                    pe.wait_ge(s_v0, B)
                if m == 3:
                    pe.wait_ge(s_parts, B)
                bank = banks(KV_BANK[m])
                before = [i for i in range(m) if KV_BANK[i] == KV_BANK[m]]
                if before:
                    pe.wait_ge(s_k1c, before[-1] + 1)
                elif KV_BANK[m] < 2:
                    pe.wait_ge(s_mx0, 12 * B)
                if j < 2:
                    for c in range(2):
                        last = mm(bank[:, c * S:(c + 1) * S], W1[:, 1, (2 * j + c) * P:(2 * j + c + 1) * P],
                                  CT[:, b * S:(b + 1) * S], start=True, stop=True)
                else:
                    t = 2 * b + j - 2
                    last = mm(bank, CT[:, t * P:(t + 1) * P], W1[:, 2, :], start=True, stop=True)
                last.then_inc(s_k1, 1)

            def scores0(n):
                b, u = divmod(n, 12)
                if n == 0:
                    pe.wait_ge(s_vtc, 1)
                    pe.wait_ge(d_one0, 16)
                if n == 12:
                    pe.wait_ge(d_one, 16)
                if u == 0:
                    pe.wait_ge(d_qk[b], 16 if b else 12 * 16)
                if n >= 2:
                    pe.wait_ge(s_mx0, n - 1)
                if u < 8:
                    view = banks(n % 2).rearrange("p (h j) -> p h j", h=2)
                    mm(view[:, :, P:2 * P], IDB[:, :], MSKB[:, 1:2, :].to_broadcast([P, 2, P]),
                       start=True, stop=False, skip_group_check=True)
                    for g in range(2):
                        h = 2 * u + g
                        last = mm(view[:, g, :], QKh[0:KZ, 0, b, h, P:2 * P], QKh[0:KZ, 1, b, h, :],
                                  start=False, stop=True, skip_group_check=True)
                else:
                    view = banks(n % 2).rearrange("p (h j) -> p h j", h=4)
                    mm(view, IDB[:, :], MSKB[:, 0:1, :].to_broadcast([P, 4, P]),
                       start=True, stop=False, skip_group_check=True)
                    for g in range(4):
                        h = 4 * (u - 8) + g
                        last = mm(view[:, g, :], QKh[0:KZ, 0, b, h, 0:P], QKh[0:KZ, 1, b, h, 0:P],
                                  start=False, stop=True, skip_group_check=True)
                last.then_inc(s_s0, 1)

            pe.wait_ge(s_cst, 1)

            def scores0T(n):
                b, hg = divmod(n, 4)
                if hg == 0:
                    pe.wait_ge(d_shift[b], 16)
                if n == 0:
                    pe.wait_ge(s_k1c, 4 * B - KV_LATE)
                    pe.wait_ge(s_vpc, ELT)
                else:
                    pe.wait_ge(s_pa, n)
                for g in range(4):
                    h = 4 * hg + g
                    last = mm(banks(2, 1024)[:, g * S:(g + 1) * S], QKh[0:KZ, 1, b, h, 0:P],
                              QKh[0:KZ, 0, b, h, :], start=True, stop=True)
                last.then_inc(s_sta, 1)
                if n >= 1:
                    pe.wait_ge(s_p0, n)
                for g in range(4):
                    h = 4 * hg + g
                    last = mm(banks(4)[:, g * P:(g + 1) * P], QKh[0:KZ, 1, b, h, P:2 * P],
                              QKh[0:KZ, 0, b, h, P:2 * P], start=True, stop=True)
                last.then_inc(s_stb, 1)

            def outputs0(n):
                b, hg = divmod(n, 4)
                if n == 0:
                    pe.wait_ge(s_v0, B)
                    pe.wait_ge(s_va0, 1)
                pe.wait_ge(s_pm, n + 1)
                if n >= 2 and n % 2 == 0:
                    pe.wait_ge(s_ots, n // 2)
                half = n % 2 * S
                for jt in range(2):
                    for g in range(4):
                        rows = slice(32 * g, 32 * g + 32)
                        src = PT0[:, n % 3, g, 0:256] if jt == 0 else PT0[:, n % 3, g, 256:384]
                        last = mm(banks(5)[rows, half + jt * P:half + S], VA[:, 2 * b + jt, 4 * hg + g, :], src,
                                  start=(jt == 0), stop=(jt == 1), skip_group_check=True)
                last.then_inc(s_av0, 1)

            def transpose_heads(pp):
                pe.wait_ge(s_ots, pp + 1)
                if pp >= 1:
                    pe.wait_ge(s_od, pp)
                for it in range(2):
                    for q in range(2):
                        last = nc.tensor.transpose(banks(6)[:, (2 * it + q) * P:(2 * it + q + 1) * P],
                                                   OTS[:, pp % 2, q * S + it * P:q * S + (it + 1) * P], ident)
                last.then_inc(s_ott, 1)

            def logits(n):
                if n == 0:
                    pe.wait_ge(s_p0, 4 * B)
                    pe.wait_ge(s_k1c, 4 * B)
                if n >= 2:
                    pe.wait_ge(s_te, n - 1)
                pe.wait_ge(s_xt, B + n // 2 + 1)
                xt = XT[:, n * P:(n + 1) * P]
                mm(banks(2 * (n % 2), 300), xt, TG[:, 0:300], start=True, stop=True)
                mm(banks(2 * (n % 2) + 1, 300), xt, TG[:, 306:606], start=True, stop=True).then_inc(s_lg, 1)

            def transpose_te(n):
                pe.wait_ge(s_pe, n + 1)
                if n == 0:
                    pe.wait_ge(s_ots, 2 * B)
                else:
                    pe.wait_ge(s_ptec, n)
                for t in range(ELT):
                    last = nc.tensor.transpose(banks(4, 640)[0:EL, t * P:(t + 1) * P],
                                               TE[:, n % 3, t * EL:(t + 1) * EL], ident)
                last.then_inc(s_pte, 1)

            def values(n):
                if n == 0:
                    pe.wait_ge(s_od, 2 * B)
                else:
                    pe.wait_ge(s_dl, n)
                acc = banks(6)
                mm(acc[:, D:2 * D], XT[:, n * P:(n + 1) * P], WTD[:, 1, :], start=True, stop=True)
                pe.wait_ge(s_ptec, n + 1)
                for t in range(ELT):
                    last = mm(acc[:, 0:D], PTE[:, n % 2, t, :], VP[:, t, :], start=(t == 0),
                              stop=(t == ELT - 1), skip_group_check=True)
                last.then_inc(s_acc, 1)

            def scores1(n):
                b, c = divmod(n, 4)
                pe.wait_ge(s_q1, 2 * b + c // 2 + 1)
                if n == 0:
                    pe.wait_ge(s_te, NT)
                if n >= 2:
                    pe.wait_ge(s_e1, n - 1)
                for h in range(2):
                    for it in range(2):
                        last = mm(banks(2 * (n % 2) + h)[:, it * S:(it + 1) * S],
                                  QT1[:, c, h, it * P:(it + 1) * P], KT1[:, c, b * S:(b + 1) * S],
                                  start=True, stop=True)
                last.then_inc(s_s1, 1)

            def transpose_p(n):
                pe.wait_ge(s_p1, n + 1)
                pe.wait_ge(s_p1p, n + 1)
                if n == 0:
                    pe.wait_ge(s_ptec, NT)
                else:
                    pe.wait_ge(s_pt1a, n)
                    pe.wait_ge(s_pt1d, n)
                for h in range(2):
                    for jt in range(2):
                        for it in range(2):
                            last = nc.tensor.transpose(
                                banks(4 + h)[:, jt * S + it * P:jt * S + (it + 1) * P],
                                PR[:, n % 3, h, it, jt * P:(jt + 1) * P], ident)
                last.then_inc(s_t1, 1)

            def outputs1(n):
                b, c = divmod(n, 4)
                if n == 0:
                    pe.wait_ge(s_dl, NT)
                pe.wait_ge(s_pt1a, n + 1)
                pe.wait_ge(s_pt1d, n + 1)
                if n >= 2 and n % 2 == 0:
                    pe.wait_ge(s_ot1, n // 2)
                for jt in range(2):
                    for h in range(2):
                        rows = slice(64 * h, 64 * h + 64)
                        last = mm(banks(6)[rows, (n % 2) * S:(n % 2 + 1) * S],
                                  V1[:, 2 * b + jt, (2 * c + h) * D1:(2 * c + h + 1) * D1],
                                  PT1[:, n % 3, h, jt, :], start=(jt == 0), stop=(jt == 1), skip_group_check=True)
                last.then_inc(s_av1, 1)

            def hidden(m):
                b, k = divmod(m, 2)
                if k == 0:
                    pe.wait_ge(d_w12[b], 32)
                if m == 0:
                    pe.wait_ge(s_e1, 4 * B)
                if m >= 2:
                    pe.wait_ge(s_g, m - 1)
                for f in range(FT):
                    last = mm(banks(2 * (m % 2), 1024)[:, f * S:(f + 1) * S], W12[:, m, f * P:(f + 1) * P],
                              XT[:, b * S:(b + 1) * S], start=True, stop=True)
                last.then_inc(s_h, 1)

            def expert_out(m):
                b, k = divmod(m, 2)
                if m == 0:
                    pe.wait_ge(s_pt1a, 4 * B)
                    pe.wait_ge(s_pt1d, 4 * B)
                if m >= 2:
                    pe.wait_ge(s_yc, m - 1)
                pe.wait_ge(s_g, m + 1)
                for t in range(2):
                    for f in range(FT):
                        last = mm(banks(4 + k)[:, t * P:(t + 1) * P],
                                  HT[:, m % 2, f, t * P:(t + 1) * P], W12[:, m, F + f * P:F + (f + 1) * P],
                                  start=(f == 0), stop=(f == FT - 1))
                last.then_inc(s_y, 1)

            def event(ev):
                kind, b = ev[0], ev[-1]
                if kind == "xT":
                    transpose_x(ev[1], b)
                    return
                take_misc(*ev)
                if kind == "mT":
                    pe.wait_ge(s_mparts, b + 1)
                    out16 = misc[0:32, 0:128].bitcast(bf16)
                    for it in range(2):
                        last = nc.tensor.transpose(out16[:, it * P:(it + 1) * P],
                                                   MP[:, b, it].rearrange("p k h -> p (k h)"), IDB[:, :])
                elif kind == "oT":
                    pe.wait_ge(s_od, 2 * b + 2)
                    for it in range(2):
                        last = nc.tensor.transpose(misc[:, it * P:(it + 1) * P], OD[:, b % 2, it, :], ident)
                elif kind == "wo0":
                    pe.wait_ge(s_odt, b + 1)
                    if b == 0:
                        pe.wait_ge(d_late, 64)
                    for it in range(2):
                        last = mm(misc[:, S + it * P:S + (it + 1) * P], ODT[:, b % 2, it * P:(it + 1) * P],
                                  WO0[:, :], start=True, stop=True)
                elif kind == "gate":
                    pe.wait_ge(s_xt, B + b + 1)
                    for t in range(2):
                        last = mm(misc[:, t * NX:(t + 1) * NX], XT[:, b * S + t * P:b * S + (t + 1) * P],
                                  TG[:, 300:306], start=True, stop=True)
                elif kind == "q":
                    b, j = ev[1], ev[2]
                    pe.wait_ge(s_xt, 2 * B + b + 1)
                    for c in range(2):
                        last = mm(misc[:, c * S:(c + 1) * S], W1[:, 0, (2 * j + c) * P:(2 * j + c + 1) * P],
                                  XT[:, b * S:(b + 1) * S], start=True, stop=True)
                elif kind == "wo1":
                    pe.wait_ge(s_ot1, 2 * b + 2)
                    for it in range(2):
                        for c in range(4):
                            last = mm(misc[:, it * P:(it + 1) * P], OT1[:, b % 2, c, it * P:(it + 1) * P],
                                      WO1[:, c, :], start=(c == 0), stop=(c == 3))
                elif kind == "r1":
                    pe.wait_ge(s_xt, 3 * B + b + 1)
                    last = mm(misc[:, 0:NE], MS[:, b:b + 1].to_broadcast([P, P]), WR[:, :], start=True, stop=True)
                elif kind == "r2":
                    pe.wait_ge(s_oh, b + 1)
                    for k in range(3):
                        last = nc.tensor.transpose(misc[0:NE, k * P:(k + 1) * P], OH[:, b, k, :], ident)
                elif kind == "r3":
                    pe.wait_ge(s_oht, b + 1)
                    for f in range(FT):
                        last = mm(misc[:, 2 * f:2 * f + 2], B12[:, f * P:(f + 1) * P], OHT[:, b, 0:2, 0],
                                  start=True, stop=True)
                elif kind == "base":
                    pe.wait_ge(s_oht, b + 1)
                    for t in range(2):
                        last = mm(misc[:, t * P:(t + 1) * P], OHT[:, b, 2, :], B12[:, F:F + P], start=True, stop=True)
                last.then_inc(s_mp7, 1)

            for g in STEPS:
                n = g - A1
                if g < M0 + 4 * B:
                    scores0(3 * (g - M0))
                    scores0(3 * (g - M0) + 1)
                if 0 <= g < 4 * B:
                    scores0T(g)
                if E0 <= g < E0 + NT:
                    logits(g - E0)
                if 0 <= n < 4 * B:
                    scores1(n)
                if M1 <= g < M1 + 2 * B:
                    hidden(g - M1)
                for ev in events(g, 0):
                    if ev[0] in ON_PE:
                        event(ev)
                if g == M0:
                    expert_tokens(2)
                for m in kvs(g):
                    kv(m)
                if g < M0 + 4 * B:
                    scores0(3 * (g - M0) + 2)
                if 2 <= g < 4 * B + 2:
                    outputs0(g - 2)
                if g >= 4 and g % 2 == 0 and (g - 4) // 2 < 2 * B:
                    transpose_heads((g - 4) // 2)
                if E0 + 2 <= g < E0 + 2 + NT:
                    transpose_te(g - E0 - 2)
                if E0 + 3 <= g < E0 + 3 + NT:
                    values(g - E0 - 3)
                if 2 <= n < 4 * B + 2:
                    transpose_p(n - 2)
                if 3 <= n < 4 * B + 3:
                    outputs1(n - 3)
                if M1 + 1 <= g < M1 + 1 + 2 * B:
                    expert_out(g - M1 - 1)
                for ev in events(g, 1):
                    if ev[0] in ON_PE:
                        event(ev)


def kernel(**inputs):
    import numpy as np
    import concourse.bacc as bacc
    from concourse.bass_utils import run_bass_kernel_spmd

    i = {k: np.asarray(v) for k, v in inputs.items()}
    cat = np.concatenate
    fp = np.float32
    c = np.zeros((P, NCONST), fp)
    c[:, C_ID:C_ID + P] = np.eye(P, dtype=fp)
    row, col = np.mgrid[0:P, 0:P]
    for it in range(2):
        keep = (col < row) | ((row == 0) & (col == 0) & (it == 0))
        c[:, C_MASK + it * P:C_MASK + (it + 1) * P] = np.where(keep, fp(0), fp(-BIG))
    flat = np.arange(EL)[:, None] + EL * np.arange(ELT)[None, :]
    c[:EL, C_L0:C_L0 + ELT] = (flat % NL != 0).astype(fp)
    c[:, C_W6:C_W6 + 6] = np.arange(NX, 0, -1, dtype=fp)
    c[:, C_IOTA:C_IOTA + NE] = np.arange(NE, dtype=fp)
    by_feature = lambda w: w.reshape(D, H0, D0).transpose(0, 2, 1).reshape(D, D)
    arrays = {
        "x": i["x"].reshape(B * S, D),
        "ctxT": i["ctx_1024"].reshape(B * S, D).T,
        "w0": np.stack([by_feature(i["L0_xattn_W_q"]), by_feature(i["L0_xattn_W_k"]), i["L0_xattn_W_v"]], 1),
        "wo0": i["L0_xattn_W_o"],
        "ab": cat([i["L0_ffn_A"].transpose(2, 0, 1).reshape(NR, NX * NL),
                   i["L0_ffn_B"].transpose(1, 0, 2).reshape(NR, NX * D)], 1),
        "wtd": np.stack([i["L0_ffn_wt_w"].T, i["L0_ffn_wd_w"].T], 1),
        "wgate": i["L0_ffn_w_gate"],
        "vecs": cat([np.stack([i["g_xattn"], i["g_ffn"]], 0).reshape(4)[[0, 1, 2, 3]], i["L0_xattn_b_o"],
                     i["L1_xattn_bo"], i["L0_ffn_wd_b"], i["L1_ffn_gamma"], i["L1_ffn_beta"],
                     i["L1_ffn_br"], i["L0_ffn_scale"]]),
        "cols": np.stack([i["L0_xattn_b_v"], i["L0_ffn_wt_b"]], 1),
        "w1": np.stack([i["L1_xattn_Wq"], i["L1_xattn_Wk"], i["L1_xattn_Wv"]], 1),
        "wo1": i["L1_xattn_Wo"].reshape(4, P, D).transpose(1, 0, 2),
        "wr": i["L1_ffn_Wr"],
        "b12": cat([i["L1_ffn_b1"], i["L1_ffn_b2"]], 1),
        "w12": cat([i["L1_ffn_W1"],
                    i["L1_ffn_W2"].reshape(NE, FT, P, D).transpose(0, 2, 1, 3).reshape(NE, P, F)], 2),
        "consts": c,
    }
    nc = bacc.Bacc("TRN2", target_bir_lowering=False, num_devices=1)
    feed, args = {}, []
    for name, a in arrays.items():
        a = np.ascontiguousarray(a)
        feed["in_" + name] = a
        args.append(nc.dram_tensor("in_" + name, a.shape, mybir.dt.from_np(a.dtype), kind="ExternalInput").ap())
    args.append(nc.dram_tensor("out_x", (B * S, D), mybir.dt.float32, kind="ExternalOutput").ap())
    args.append(nc.dram_tensor("qk_scr", (B, 2, 6, P, S), mybir.dt.bfloat16, kind="Internal").ap())
    build_program(nc, *args)
    r = run_bass_kernel_spmd(nc, [feed], core_ids=[0])
    return r.results[0]["out_x"].reshape(B, S, D)
```
